# Optimizing a Trainium2 kernel written in Bass

```python
import numpy as np
import jax
import jax.numpy as jnp

def _softmax(x, axis=-1):
    return jax.nn.softmax(x, axis=axis)

def _gelu(x):
    return jax.nn.gelu(x, approximate=True)

def _silu(x):
    return jax.nn.silu(x)

def _sigmoid(x):
    return jax.nn.sigmoid(x)

def _layernorm(x, axis=-1, eps=1e-05):
    m = jnp.mean(x, axis=axis, keepdims=True)
    v = jnp.var(x, axis=axis, keepdims=True)
    return (x - m) / jnp.sqrt(v + eps)

def _scatter_add(tgt, idx, src, axis=0):
    return tgt.at[idx].add(src)

def _segment_sum(src, seg, n):
    return jax.ops.segment_sum(src, seg, n)
kernel_name = 'mk_xattn_ffn_d1_seqx_r8_ec91f8'

def setup_inputs(seed: int=0):
    np.random.seed(seed)
    _w = jnp.asarray

    def _rec_inputs():
        import jax
        import jax.numpy as jnp
        _rk = jax.random.key(seed)
        x = 7.22e-05 + 1 * jax.random.normal(jax.random.fold_in(_rk, 1), (8, 128, 512), jnp.float32)
        _lenS = 128 - jax.random.randint(jax.random.fold_in(_rk, 7), (8,), 0, max(1, 128 // 4) + 1, jnp.int32)
        _lenS2 = 128 - jax.random.randint(jax.random.fold_in(_rk, 8), (8,), 0, max(1, 128 // 4) + 1, jnp.int32)
        _ctx_4096P = jax.random.normal(jax.random.fold_in(_rk, 11), (8, 16, 512), jnp.float32)
        _ctx_4096c = jax.random.dirichlet(jax.random.fold_in(_rk, 511), 0.3 * jnp.ones((16,), jnp.float32), (8, 128))
        _ctx_4096t = jnp.einsum('bsk,bkd->bsd', _ctx_4096c, _ctx_4096P)
        _ctx_4096t = _ctx_4096t * jax.lax.rsqrt(jnp.mean(jnp.square(_ctx_4096t)) + 1e-12) * 0.953939
        ctx_4096 = 4.13588e-05 + 0.999923 * (_ctx_4096t + 0.3 * jax.random.normal(jax.random.fold_in(_rk, 611), (8, 128, 512), jnp.float32))
        return (x, ctx_4096)
    x, ctx_4096 = _rec_inputs()

    def _L0_xattn_setup():
        import jax, jax.numpy as jnp
        import numpy as np
        import math
        D_MODEL = 128
        NHEAD = 16
        MAX_SUP = 4
        DK = D_MODEL // NHEAD
        DM = D_MODEL * MAX_SUP
        B, S = (2, 128)
        key = jax.random.key(seed)
        ks = jax.random.split(key, 12)
        std = 0.02
        inp = {'q': jax.random.normal(ks[0], (B, S, DM), jnp.float32), 'k': jax.random.normal(ks[1], (B, S, DM), jnp.float32), 'v': jax.random.normal(ks[2], (B, S, DM), jnp.float32), 'Wq': jax.random.normal(ks[3], (DM, DM), jnp.float32) * std, 'bq': jnp.zeros((DM,), jnp.float32), 'Wk': jax.random.normal(ks[4], (DM, DM), jnp.float32) * std, 'bk': jnp.zeros((DM,), jnp.float32), 'Wv': jax.random.normal(ks[5], (DM, DM), jnp.float32) * std, 'bv': jnp.zeros((DM,), jnp.float32), 'interference': jax.random.normal(ks[6], (NHEAD, MAX_SUP, MAX_SUP), jnp.float32), 'amp': jnp.ones((1,), jnp.float32), 'Wo': jax.random.normal(ks[7], (DM, DM), jnp.float32) * std, 'bo': jnp.zeros((DM,), jnp.float32)}
        return inp
    _L0_xattn_all = _L0_xattn_setup()
    _L0_xattn_in = {k: v for k, v in _L0_xattn_all.items() if k in ('Wq', 'bq', 'Wk', 'bk', 'Wv', 'bv', 'interference', 'amp', 'Wo', 'bo')}
    del _L0_xattn_all

    def _L0_ffn_setup():
        import jax, jax.numpy as jnp
        import numpy as np
        D_MODEL = 512
        D_FF = 1376
        key = jax.random.key(seed)
        k1, k2, k3, k4 = jax.random.split(key, 4)
        x = jax.random.normal(k1, (2, 256, D_MODEL), dtype=jnp.float32)
        W_gate = jax.random.normal(k2, (D_FF, D_MODEL), dtype=jnp.float32) * D_MODEL ** (-0.5)
        W_up = jax.random.normal(k3, (D_FF, D_MODEL), dtype=jnp.float32) * D_MODEL ** (-0.5)
        W_down = jax.random.normal(k4, (D_MODEL, D_FF), dtype=jnp.float32) * D_FF ** (-0.5)
        return {'x': x, 'W_gate': W_gate, 'W_up': W_up, 'W_down': W_down}
    _L0_ffn_all = _L0_ffn_setup()
    _L0_ffn_in = {k: v for k, v in _L0_ffn_all.items() if k in ('W_gate', 'W_up', 'W_down')}
    del _L0_ffn_all
    return {'x': x, 'ctx_4096': ctx_4096, 'L0_xattn_Wq': _L0_xattn_in['Wq'], 'L0_xattn_bq': _L0_xattn_in['bq'], 'L0_xattn_Wk': _L0_xattn_in['Wk'], 'L0_xattn_bk': _L0_xattn_in['bk'], 'L0_xattn_Wv': _L0_xattn_in['Wv'], 'L0_xattn_bv': _L0_xattn_in['bv'], 'L0_xattn_interference': _L0_xattn_in['interference'], 'L0_xattn_amp': _L0_xattn_in['amp'], 'L0_xattn_Wo': _L0_xattn_in['Wo'], 'L0_xattn_bo': _L0_xattn_in['bo'], 'L0_ffn_W_gate': _L0_ffn_in['W_gate'], 'L0_ffn_W_up': _L0_ffn_in['W_up'], 'L0_ffn_W_down': _L0_ffn_in['W_down']}

def reference(x, ctx_4096, L0_xattn_Wq, L0_xattn_bq, L0_xattn_Wk, L0_xattn_bk, L0_xattn_Wv, L0_xattn_bv, L0_xattn_interference, L0_xattn_amp, L0_xattn_Wo, L0_xattn_bo, L0_ffn_W_gate, L0_ffn_W_up, L0_ffn_W_down):
    import jax
    import jax.numpy as jnp

    def _L0_xattn_ref(q, k, v, Wq, bq, Wk, bk, Wv, bv, interference, amp, Wo, bo):
        import jax, jax.numpy as jnp
        import numpy as np
        import math
        D_MODEL = 128
        NHEAD = 16
        MAX_SUP = 4
        DK = D_MODEL // NHEAD
        DM = D_MODEL * MAX_SUP
        B, S = (2, 128)
        b, s, dm = q.shape
        H, M = (interference.shape[0], interference.shape[1])
        dk = dm // (H * M)

        def proj(x, W, bias):
            y = x @ W.T + bias
            y = y.reshape(b, s, H, dk, M)
            return jnp.transpose(y, (0, 2, 1, 3, 4))
        qh = proj(q, Wq, bq)
        kh = proj(k, Wk, bk)
        vh = proj(v, Wv, bv)

        def interfere(x):
            return x + 0.1 * amp[0] * jnp.einsum('bhsdi,hij->bhsdj', x, interference)
        qh, kh, vh = (interfere(qh), interfere(kh), interfere(vh))
        scores = jnp.einsum('bhqdm,bhkdm->bhqkm', qh, kh) / math.sqrt(dk)
        weights = jax.nn.softmax(scores, axis=3)
        out = jnp.einsum('bhqkm,bhkdm->bhqdm', weights, vh)
        out = jnp.transpose(out, (0, 2, 1, 3, 4)).reshape(b, s, dm)
        return out @ Wo.T + bo

    def _L0_ffn_ref(x, W_gate, W_up, W_down):
        import jax, jax.numpy as jnp
        import numpy as np
        D_MODEL = 512
        D_FF = 1376
        out_shape = x.shape[:-1] + (W_down.shape[0],)
        xf = x.reshape(-1, x.shape[-1])
        up = jnp.einsum('td,fd->tf', xf, W_up)
        gate = jax.nn.silu(jnp.einsum('td,fd->tf', xf, W_gate))
        h = gate * up
        y = jnp.einsum('tf,df->td', h, W_down)
        return y.reshape(out_shape)
    x = x + _L0_xattn_ref(_layernorm(x, axis=-1), ctx_4096, ctx_4096, L0_xattn_Wq, L0_xattn_bq, L0_xattn_Wk, L0_xattn_bk, L0_xattn_Wv, L0_xattn_bv, L0_xattn_interference, L0_xattn_amp, L0_xattn_Wo, L0_xattn_bo)
    x = x + _L0_ffn_ref(_layernorm(x, axis=-1), L0_ffn_W_gate, L0_ffn_W_up, L0_ffn_W_down)
    return x

_drawn_inputs = setup_inputs


def setup_inputs(seed=0):
    import zlib

    import numpy as np

    out = dict(_drawn_inputs(seed))
    spreads = {'L0_xattn_bq': (0.0, 0.8),
     'L0_xattn_bk': (0.0, 0.8),
     'L0_xattn_bv': (0.0, 0.1),
     'L0_xattn_bo': (0.0, 0.1)}
    factors = {'L0_xattn_Wq': 5.788, 'L0_xattn_Wk': 5.632}
    for name, (base, spread) in spreads.items():
        noise = np.random.default_rng([zlib.crc32(name.encode()), seed]).standard_normal(out[name].shape)
        drawn = base * np.exp(spread * noise) if base else spread * noise
        out[name] = jnp.asarray(drawn.astype(out[name].dtype))
    for name, factor in factors.items():
        out[name] = (out[name] * factor).astype(out[name].dtype)
    return out
```

```python
import concourse.bass as bass
from concourse import mybir
from contextlib import ExitStack

F32 = mybir.dt.float32
F32R = mybir.dt.float32r
ACT = mybir.ActivationFunctionType
ALU = mybir.AluOpType
AX = mybir.AxisListType

P = 128
B, S, D = 8, 128, 512
H, M, DK = 16, 4, 8
KB = D // P
GH = H // KB
F = 1376
FB = -(-F // P)
EPS = 1e-5
PARTS = 3
ROWS = M * PARTS * DK
PER = 3
REG = -(-H // PER)
LAG_B = 12
LAG_V = LAG_B + 2
HALF = H // 2
PTN = 3
TOK = 512
KW, QW, VW = range(3)


def plan():
    at = {}

    def place(step, *job):
        at.setdefault(step, []).append(job)

    for w in (KW, QW, VW):
        for k in range(KB):
            place(-17, "W", w, k)
        place(-17, "bias", w)
    for b in range(B):
        t = 16 * (b - 1)
        place(t + 0, "split_ctx", b)
        place(t + 0, "norm", b)
        place(t + 1, "proj", KW, b)
        place(t + 3, "xT", b)
        place(t + 4, "stack", KW, b)
        place(t + 6, "proj", QW, b)
        place(t + 8, "stack", QW, b)
        place(t + 15, "proj", VW, b)
        t += 16
        place(t + HALF + 1, "shift", b, 0)
        place(t + H + 1, "shift", b, 1)
        for r in range(REG):
            place(t + min(PER * r + PER, H) + LAG_V + 1, "norm_out", b, r)
        place(t + 33, "oT", b)
        place(t + 35, "out", b)
    steps = range(-17, max(at) + 1)
    return steps, at


def build(nc, x, ctxT, Wq, Wk, Wv, WoT, bq, bk, bv, bo, mix, amp, WgT, WuT, WdT, out):
    steps, at = plan()
    order = [j for g in steps for j in at.get(g, []) if j[0] not in ("split_ctx", "norm")]
    JOB = {j: n for n, j in enumerate(order)}
    HIGH = {}
    for g in steps:
        for j in at.get(g, []):
            if j[0] in ("W", "xT", "stack", "oT", "split_ctx"):
                HIGH[j] = len(HIGH)
            if j == ("bias", VW):
                HIGH["Wo"] = len(HIGH)

    with ExitStack() as ctx:
        sem = lambda n: ctx.enter_context(nc.semaphore(n))
        scr = nc.dram_tensor("stack_scratch", [2, 2, M, PARTS, DK, H, S], F32, kind="Internal").ap()
        x1d = nc.dram_tensor("x1_scratch", [B, S, D], F32, kind="Internal").ap()
        PS = ctx.enter_context(nc.psum_tensor("PS", [P, 8, 512], F32))

        def alloc(stack):
            return lambda n, s, d=F32: stack.enter_context(nc.sbuf_tensor(n, s, d))

        sb = alloc(ctx)
        ident = sb("ident", [P, P])
        neghalf = sb("neghalf", [P, 1])

        one = ExitStack()
        sb = alloc(one)
        WH = [sb(f"WH{w}", [P, KB, D], F32R) for w in range(4)]
        WL = [sb(f"WL{w}", [P, KB, D], F32R) for w in range(4)]
        bias = [sb(f"bias{w}", [P, D]) for w in range(3)]
        bob = sb("bob", [P, D])
        mask96 = sb("mask96", [ROWS, M])
        mask64 = sb("mask64", [64, M])
        sel = sb("sel", [64, HALF, P], F32R)
        Vpad = [sb(f"Vpad{i}", [P, H, M, 32]) for i in range(2)]
        prep = ExitStack()
        sbp = alloc(prep)
        Wn = [sbp(f"Wn{w}", [P, KB, D]) for w in range(4)]
        mixs = sbp("mixs", [P, KB, M])
        amps = sbp("amps", [P, 1])
        BD = sbp("BD", [P, KB, P])
        bcol = sbp("bcol", [P, 3, KB])
        bwide = sbp("bwide", [P, 3, KB, P])
        blk = sbp("blk", [P, P // M])
        selc = sbp("selc", [64, HALF])
        prep.close()
        Kst = [sb(f"Kst{i}", [ROWS, H, S], F32R) for i in range(2)]
        Qst = [sb(f"Qst{i}", [ROWS, H, S], F32R) for i in range(2)]
        Kbd = [sb(f"Kbd{i}", [ROWS, GH, M, S], F32R) for i in range(2)]
        Qbd = [sb(f"Qbd{i}", [ROWS, GH, M, S], F32R) for i in range(2)]
        xin = sb("xin", [P, D])
        xres = sb("xres", [P, D])
        cin = sb("cin", [P, KB, S])
        cH = sb("cH", [P, KB, S], F32R)
        cL = sb("cL", [P, KB, S], F32R)
        stats = sb("stats", [P, 6])
        mv = sb("mv", [P, 2])
        ve = sb("ve", [P, 1])
        rstd = sb("rstd", [P, 1])
        xTH = sb("xTH", [P, KB, S], F32R)
        xTL = sb("xTL", [P, KB, S], F32R)
        kq = [sb(f"kq{w}", [P, D]) for w in range(2)]
        kqH = [sb(f"kqH{w}", [P, M, S], F32R) for w in range(2)]
        kqL = [sb(f"kqL{w}", [P, M, S], F32R) for w in range(2)]
        mx = sb("mx", [P, M, H])
        nm = sb("nm", [P, M, 2, HALF], F32R)
        nmbd = [sb(f"nmbd{i}", [64, M, S], F32R) for i in range(2)]
        PT = [sb(f"PT{i}", [P, M, S]) for i in range(PTN)]
        reg = [sb(f"reg{i}", [P, S]) for i in range(2)]
        rec = sb("rec", [P, M, PER])
        on = sb("on", [P, D])
        oTH = sb("oTH", [P, KB, S], F32R)
        oTL = sb("oTL", [P, KB, S], F32R)
        x1 = sb("x1", [P, D])
        one.close()

        two = ExitStack()
        sb = alloc(two)
        gH, gL, uH, uL = [sb(n, [P, KB, F], F32R) for n in ("gH", "gL", "uH", "uL")]
        dH, dL = [sb(n, [P, FB, D], F32R) for n in ("dH", "dL")]
        x2H, x2L = [sb(n, [P, KB, B * S], F32R) for n in ("x2H", "x2L")]
        fin = [sb(f"fin{i}", [P, D]) for i in range(3)]
        x1in = [sb(f"x1in{i}", [P, D]) for i in range(2)]
        stats2 = sb("stats2", [P, 6])
        mv2 = sb("mv2", [P, 2])
        ve2 = sb("ve2", [P, 1])
        rstd2 = sb("rstd2", [P, 1])
        x2n = sb("x2n", [P, D])
        th = sb("th", [P, TOK])
        hu = sb("hu", [P, TOK])
        hf = sb("hf", [P, TOK])
        hH = [sb(f"hH{i}", [P, TOK], F32R) for i in range(2)]
        hL = [sb(f"hL{i}", [P, TOK], F32R) for i in range(2)]
        yo = [sb(f"yo{i}", [P, D]) for i in range(2)]
        two.close()

        mix_in, bias_in, bo_in = [sem(n) for n in ("mix_in", "bias_in", "bo_in")]
        w_in = [sem(f"w_in{w}") for w in range(4)]
        x_in, c_in, xres_in = sem("x_in"), sem("c_in"), sem("xres_in")
        stack_written = [sem(f"stack_written{w}") for w in range(2)]
        stack_in = [[sem(f"stack_in{w}{i}") for i in range(2)] for w in range(2)]
        x1_written = sem("x1_written")
        pool_setup, dve_setup, mixed, wide = sem("pool_setup"), sem("dve_setup"), sem("mixed"), sem("wide")
        job_ready, job_done, high_done = sem("job_ready"), sem("job_done"), sem("high_done")
        low_ctx, stat, rstd_ready, xn_ready = sem("low_ctx"), sem("stat"), sem("rstd_ready"), sem("xn_ready")
        nm_ready, rec_ready, resid = sem("nm_ready"), sem("rec_ready"), sem("resid")
        a_ready, max_ready, b_ready, exp_ready, v_ready, reg_ready = [
            sem(n) for n in ("a_ready", "max_ready", "b_ready", "exp_ready", "v_ready", "reg_ready")]
        bd_built = [sem("kbd_built"), sem("qbd_built")]
        x1_in = [sem(f"x1_in{i}") for i in range(2)]
        stat2, rstd2_ready, x2n_ready, x2T_ready, x2H_ready, x2L_ready = [
            sem(n) for n in ("stat2", "rstd2_ready", "x2n_ready", "x2T_ready", "x2H_ready", "x2L_ready")]
        ffw_in, ffw_high, ffw_low = sem("ffw_in"), sem("ffw_high"), sem("ffw_low")
        g_ready, u_ready, th_ready, hu_ready, hf_ready, hH_ready, hL_ready, y_ready = [
            sem(n) for n in ("g_ready", "u_ready", "th_ready", "hu_ready", "hf_ready", "hH_ready", "hL_ready", "y_ready")]
        y_added = sem("y_added")
        out_written = [sem(f"out_written{i}") for i in range(2)]

        def since(eng, s, n):
            if n > 0:
                eng.wait_ge(s, n)

        def region_last(r):
            return min(PER * r + PER, H) - 1

        block = ctx.enter_context(nc.Block())

        @block.sync
        def _(sp):
            sp.dma_start(mixs[:, :, :], mix.rearrange("(g p) j -> p g j", p=P)).then_inc(mix_in, 16)
            sp.dma_start(amps[:, :], amp).then_inc(mix_in, 16)
            for w, (W, bb) in enumerate(((Wk, bk), (Wq, bq), (Wv, bv))):
                sp.dma_start(bcol[:, w, :], bb).then_inc(bias_in, 16)
            for w, W in enumerate((Wk, Wq, Wv)):
                sp.dma_start(Wn[w][:, :, :], W.rearrange("(g p) c -> p g c", p=P)).then_inc(w_in[w], 16)
            sp.dma_start(Wn[3][:, :, :], WoT.rearrange("(k p) n -> p k n", p=P)).then_inc(w_in[3], 16)
            sp.dma_start(bob[:, :], bo).then_inc(bo_in, 16)
            for g in steps[1:]:
                for j in at.get(g, []):
                    if j[0] == "split_ctx":
                        b = j[1]
                        since(sp, low_ctx, b)
                        sp.dma_start(cin[:, :, :], ctxT[b].rearrange("(k p) t -> p k t", p=P)).then_inc(c_in, 16)
                        if b:
                            sp.wait_ge(job_ready, JOB["xT", b - 1] + 1)
                        sp.dma_start(xin[:, :], x[b]).then_inc(x_in, 16)
                    if j[0] == "stack":
                        _, w, b = j
                        sp.wait_ge(job_done, JOB[j] + 1)
                        own = scr[w, b % 2]
                        for part, src in enumerate(((kqH, kqL, kqH), (kqH, kqH, kqL))[w]):
                            sp.dma_start(own[:, part].rearrange("m d h t -> (d h) m t"),
                                         src[w][:, :, :].bitcast(F32)).then_inc(stack_written[w], 16)
                        sp.wait_ge(stack_written[w], 16 * PARTS * (b + 1))
                        if b >= 2:
                            if w == KW:
                                sp.wait_ge(b_ready, H * (b - 1))
                            else:
                                sp.wait_ge(a_ready, H * (b - 1))
                            sp.wait_ge(bd_built[w], 4 * KB * (b - 1))
                        sp.dma_start((Kst, Qst)[w][b % 2][:, :, :].rearrange("p h t -> p (h t)").bitcast(F32),
                                     own.rearrange("m s d h t -> (m s d) (h t)")).then_inc(stack_in[w][b % 2], 16)
                    if j[0] == "oT":
                        b = j[1]
                        if b:
                            sp.wait_ge(job_done, JOB["out", b - 1] + 1)
                        sp.dma_start(xres[:, :], x[b]).then_inc(xres_in, 16)
                    if j[0] == "out":
                        b = j[1]
                        sp.wait_ge(job_done, JOB[j] + 1)
                        sp.dma_start(x1d[b], x1[:, :]).then_inc(x1_written, 16)
            sp.wait_ge(x1_written, 16 * B)

            def load_weights(j):
                mj = min(P, F - j * P)
                since(sp, ffw_low, 3 * j)
                for t, W in enumerate((WgT, WuT)):
                    sp.dma_start(fin[t][:, 0:KB * mj].rearrange("p (k f) -> p k f", k=KB),
                                 W[:, j * P:j * P + mj].rearrange("(k p) f -> p k f", p=P)).then_inc(ffw_in, 16)
                sp.dma_start(fin[2][0:mj, :], WdT[j * P:j * P + mj, :]).then_inc(ffw_in, 16)

            load_weights(0)
            for b in range(B):
                if b >= 2:
                    sp.wait_ge(x2n_ready, b - 1)
                sp.dma_start(x1in[b % 2][:, :], x1d[b]).then_inc(x1_in[b % 2], 16)
            for j in range(1, FB):
                load_weights(j)
            for b in range(B):
                if b >= 2:
                    sp.wait_ge(y_added, b - 1)
                else:
                    sp.wait_ge(x2n_ready, B)
                sp.dma_start(x1in[b % 2][:, :], x1d[b]).then_inc(x1_in[b % 2], 16)
                if b >= 1:
                    sp.wait_ge(y_added, b)
                    sp.dma_start(out[b - 1], yo[(b - 1) % 2][:, :]).then_inc(out_written[(b - 1) % 2], 16)
            sp.wait_ge(y_added, B)
            sp.dma_start(out[B - 1], yo[(B - 1) % 2][:, :]).then_inc(out_written[(B - 1) % 2], 16)
            for written in out_written:
                sp.wait_ge(written, 16 * (B // 2))

        @block.gpsimd
        def _(pool):
            pool.memset(ident[:, :], 0.0).then_inc(pool_setup, 1)
            pool.memset(neghalf[:, :], -0.5).then_inc(pool_setup, 1)
            pool.wait_ge(pool_setup, 2)
            pool.affine_select(out=ident[:, :], in_=ident[:, :], compare_op=ALU.not_equal, fill=1.0, base=0,
                               pattern=[[-1, P]], channel_multiplier=1).then_inc(pool_setup, 1)
            for v in Vpad:
                pool.memset(v[:, :, :, :], 0.0).then_inc(pool_setup, 1)
            pool.wait_ge(pool_setup, 5)
            for v in Vpad:
                for i in range(PER):
                    pool.memset(v[:, i:H:PER, :, DK * PER + i], 1.0).then_inc(pool_setup, 1)

            def spread(w, q):
                b, u = q // KB, q % KB
                pool.wait_ge(stack_in[w][b % 2], 16 * (b // 2 + 1))
                since(pool, (a_ready, b_ready)[w], GH * (q - 1))
                st, bd = ((Kst, Kbd), (Qst, Qbd))[w]
                for m in range(M):
                    pool.tensor_scalar(bd[q % 2][:, :, m, :], st[b % 2][:, GH * u:GH * u + GH, :].bitcast(F32),
                                       mask96[:, m:m + 1], 1.0, ALU.mult, ALU.mult).then_inc(bd_built[w], 1)

            def power(b):
                pool.wait_ge(stat, 3 * b + 3)
                pool.tensor_tensor(rstd[:, :], ve[:, :], neghalf[:, :], ALU.pow).then_inc(rstd_ready, 1)

            pool.wait_ge(dve_setup, 1)
            power(0)
            for q in range(KB * B + 3):
                if q < KB * B:
                    spread(0, q)
                if q % KB == 0 and q // KB + 1 < B:
                    power(q // KB + 1)
                if q >= 3:
                    spread(1, q - 3)
            for b in range(B):
                pool.wait_ge(stat2, 3 * b + 3)
                pool.tensor_tensor(rstd2[:, :], ve2[:, :], neghalf[:, :], ALU.pow).then_inc(rstd2_ready, 1)

        @block.scalar
        def _(act):
            def high(j, dst, src):
                act.activation(dst, src, ACT.Copy).then_inc(high_done, 1)

            def split_h_high(n):
                mj = min(P, F - (n % FB) * P)
                act.wait_ge(hf_ready, n + 1)
                since(act, y_ready, n - 1)
                act.activation(hH[n % 2][0:mj, :], hf[0:mj, :], ACT.Copy).then_inc(hH_ready, 1)

            for g in steps:
                for j in at.get(g, []):
                    n = JOB.get(j)
                    if j[0] == "W":
                        _, w, k = j
                        act.wait_ge(job_ready, n + 1)
                        high(j, WH[w][:, k, :].rearrange("p (m d h) -> p m d h", m=M, d=DK),
                             PS[:, 6 + n % 2, :].rearrange("p (h d m) -> p m d h", h=H, d=DK))
                    if j == ("bias", VW):
                        act.wait_ge(w_in[3], 16)
                        high("Wo", WH[3][:, :, :], Wn[3][:, :, :])
                    if j[0] == "split_ctx":
                        b = j[1]
                        act.wait_ge(c_in, 16 * (b + 1))
                        if b:
                            act.wait_ge(job_ready, JOB["proj", VW, b - 1] + 1)
                        high(j, cH[:, :, :], cin[:, :, :])
                    if j[0] == "xT":
                        act.wait_ge(job_ready, n + 1)
                        high(j, xTH[:, :, :], PS[:, 6 + n % 2, :].rearrange("p (k t) -> p k t", k=KB))
                    if j[0] == "stack":
                        _, w, b = j
                        act.wait_ge(job_ready, n + 1)
                        since(act, stack_written[w], 16 * PARTS * b)
                        high(j, kqH[w][:, :, :], PS[:, 6 + n % 2, :].rearrange("p (m t) -> p m t", m=M))
                    if j[0] == "oT":
                        act.wait_ge(job_ready, n + 1)
                        high(j, oTH[:, :, :], PS[:, 6 + n % 2, :].rearrange("p (k t) -> p k t", k=KB))
                e = g - LAG_B
                if 0 <= e < B * H:
                    act.wait_ge(b_ready, e + 1)
                    since(act, v_ready, e - PTN + 1)
                    act.activation(PT[e % PTN][:, :, :], PS[:, 2 + e % 2, :].rearrange("p (m t) -> p m t", m=M),
                                   ACT.Exp, scale=DK ** -0.5).then_inc(exp_ready, 1)
                b, h = divmod(g - LAG_V - 1, H)
                if 0 <= b < B and h in [region_last(r) for r in range(REG)]:
                    rg = REG * b + h // PER
                    act.wait_ge(v_ready, H * b + h + 1)
                    if rg >= 2:
                        act.wait_ge(job_ready, JOB["norm_out", (rg - 2) // REG, (rg - 2) % REG] + 1)
                    act.activation(reg[rg % 2][:, :], PS[:, 4 + rg % 2, 0:S], ACT.Copy).then_inc(reg_ready, 1)
            for b in range(B):
                act.wait_ge(x2T_ready, b + 1)
                act.activation(x2H[:, :, b * S:b * S + S], PS[:, b % 4, :].rearrange("p (k t) -> p k t", k=KB),
                               ACT.Copy).then_inc(x2H_ready, 1)
            for n in range(2 * FB):
                j = n % FB
                mj = min(P, F - j * P)
                if n < FB:
                    act.wait_ge(ffw_in, 48 * (j + 1))
                    for t, W in enumerate((gH, uH)):
                        act.activation(W[:, :, j * P:j * P + mj],
                                       fin[t][:, 0:KB * mj].rearrange("p (k f) -> p k f", k=KB),
                                       ACT.Copy).then_inc(ffw_high, 1)
                    act.activation(dH[0:mj, j, :], fin[2][0:mj, :], ACT.Copy).then_inc(ffw_high, 1)
                if n >= 1:
                    split_h_high(n - 1)
                act.wait_ge(g_ready, n + 1)
                since(act, hu_ready, n)
                act.activation(th[0:mj, :], PS[0:mj, 4 + n % 2, :], ACT.Tanh, scale=0.5).then_inc(th_ready, 1)
            split_h_high(2 * FB - 1)

        @block.vector
        def _(dve):
            dve.wait_ge(pool_setup, 3)
            dve.tensor_reduce(mask96[:, :], ident[0:ROWS, 0:ROWS].rearrange("p (m j) -> p m j", m=M),
                              AX.X, ALU.add).then_inc(dve_setup, 1)
            dve.tensor_reduce(mask64[:, :], ident[0:64, 0:64].rearrange("p (m j) -> p m j", m=M),
                              AX.X, ALU.add).then_inc(dve_setup, 1)
            dve.tensor_reduce(selc[:, :], ident[0:64, 0:64].rearrange("p (j h) -> p h j", h=HALF),
                              AX.X, ALU.add).then_inc(dve_setup, 1)
            dve.tensor_reduce(blk[:, :], ident[:, :].rearrange("p (k j) -> p k j", j=M),
                              AX.X, ALU.add).then_inc(dve_setup, 1)
            dve.wait_ge(dve_setup, 4)
            dve.tensor_copy(sel[:, :, :], selc[:, :].unsqueeze(2).broadcast_to([64, HALF, P])).then_inc(dve_setup, 1)
            dve.wait_ge(mix_in, 32)
            dve.tensor_scalar(mixs[:, :, :], mixs[:, :, :], amps[:, 0:1], 0.1, ALU.mult, ALU.mult).then_inc(mixed, 1)
            dve.wait_ge(mixed, 1)
            for g in range(KB):
                dve.tensor_tensor(BD[:, g, :].rearrange("p (k j) -> p k j", j=M),
                                  mixs[:, g, :].unsqueeze(1).broadcast_to([P, P // M, M]),
                                  blk[:, :].unsqueeze(2).broadcast_to([P, P // M, M]), ALU.mult).then_inc(mixed, 1)
            dve.wait_ge(mixed, 1 + KB)
            for g in range(KB):
                dve.tensor_tensor(BD[:, g, :], BD[:, g, :], ident[:, :], ALU.add).then_inc(mixed, 1)
            dve.wait_ge(bias_in, 48)
            dve.tensor_copy(bwide[:, :, :, :].rearrange("p w g t -> p (w g) t"),
                            bcol[:, :, :].rearrange("p w g -> p (w g)").unsqueeze(2).broadcast_to([P, 3 * KB, P])
                            ).then_inc(wide, 1)

            def low(j, dst, src, hi):
                dve.wait_ge(high_done, HIGH[j] + 1)
                return dve.tensor_tensor(dst, src, hi.bitcast(F32), ALU.subtract)

            for g in steps:
                if 0 <= g < B * H:
                    b, h = divmod(g, H)
                    dve.wait_ge(a_ready, g + 1)
                    dve.tensor_reduce(mx[:, :, h], PS[:, g % 2, :].rearrange("p (m t) -> p m t", m=M),
                                      AX.X, ALU.max, negate=True).then_inc(max_ready, 1)
                for j in at.get(g, []):
                    n = JOB.get(j)
                    ps = None if n is None else PS[:, 6 + n % 2, :]
                    if j[0] == "W":
                        _, w, k = j
                        low(j, WL[w][:, k, :].rearrange("p (m d h) -> p m d h", m=M, d=DK),
                            ps.rearrange("p (h d m) -> p m d h", h=H, d=DK),
                            WH[w][:, k, :].rearrange("p (m d h) -> p m d h", m=M, d=DK)).then_inc(job_done, 1)
                    if j[0] == "bias":
                        dve.wait_ge(job_ready, n + 1)
                        dve.tensor_copy(bias[j[1]][:, :].rearrange("p (m d h) -> p m d h", m=M, d=DK),
                                        ps.rearrange("p (h d m) -> p m d h", h=H, d=DK)).then_inc(job_done, 1)
                        if j[1] == VW:
                            low("Wo", WL[3][:, :, :], Wn[3][:, :, :], WH[3][:, :, :]).then_inc(wide, 1)
                    if j[0] == "split_ctx":
                        low(j, cL[:, :, :], cin[:, :, :], cH[:, :, :]).then_inc(low_ctx, 1)
                    if j[0] == "norm":
                        b = j[1]
                        dve.wait_ge(x_in, 16 * (b + 1))
                        dve.bn_stats(stats[:, :], xin[:, :]).then_inc(stat, 1)
                        dve.wait_ge(stat, 3 * b + 1)
                        dve.bn_aggr(mv[:, :], stats[:, :]).then_inc(stat, 1)
                        dve.wait_ge(stat, 3 * b + 2)
                        dve.tensor_scalar(ve[:, :], mv[:, 1:2], EPS, None, ALU.add).then_inc(stat, 1)
                    if j[0] == "proj" and j[1] == KW:
                        b = j[2]
                        dve.wait_ge(rstd_ready, b + 1)
                        dve.tensor_scalar(xin[:, :], xin[:, :], mv[:, 0:1], rstd[:, 0:1],
                                          ALU.subtract, ALU.mult).then_inc(xn_ready, 1)
                    if j[0] == "proj" and j[1] != VW:
                        dve.wait_ge(job_ready, n + 1)
                        dve.tensor_tensor(kq[j[1]][:, :], ps, bias[j[1]][:, :], ALU.add).then_inc(job_done, 1)
                    if j[0] == "proj" and j[1] == VW:
                        b = j[2]
                        dve.wait_ge(job_ready, n + 1)
                        dve.wait_ge(pool_setup, 11)
                        since(dve, v_ready, H * (b - 1))
                        for i in range(PER):
                            last = dve.tensor_tensor(
                                Vpad[b % 2][:, i:H:PER, :, DK * i:DK * i + DK],
                                ps.rearrange("p (m d h) -> p h m d", m=M, d=DK)[:, i:H:PER],
                                bias[VW][:, :].rearrange("p (m d h) -> p h m d", m=M, d=DK)[:, i:H:PER], ALU.add)
                        last.then_inc(job_done, 1)
                    if j[0] == "xT":
                        low(j, xTL[:, :, :], ps.rearrange("p (k t) -> p k t", k=KB), xTH[:, :, :]
                            ).then_inc(job_done, 1)
                    if j[0] == "stack":
                        w = j[1]
                        low(j, kqL[w][:, :, :], ps.rearrange("p (m t) -> p m t", m=M), kqH[w][:, :, :]
                            ).then_inc(job_done, 1)
                    if j[0] == "shift":
                        _, b, half = j
                        k = 2 * b + half
                        dve.wait_ge(job_ready, n + 1)
                        since(dve, b_ready, HALF * (k - 1))
                        for m in range(M):
                            last = dve.tensor_scalar(nmbd[k % 2][:, m, :], ps[0:64, 0:S], mask64[:, m:m + 1], None,
                                                     ALU.mult)
                        last.then_inc(job_done, 1)
                    if j[0] == "norm_out":
                        _, b, r = j
                        k = min(PER, H - PER * r)
                        dve.wait_ge(job_ready, n + 1)
                        if b or r:
                            dve.wait_ge(job_done, JOB["norm_out", (REG * b + r - 1) // REG, (r - 1) % REG] + 1)
                        cols = ps[:, 0:P].rearrange("p (m c) -> p m c", m=M)
                        dve.reciprocal(rec[:, :, 0:k], cols[:, :, DK * PER:DK * PER + k]).then_inc(rec_ready, 1)
                        dve.wait_ge(rec_ready, REG * b + r + 1)
                        c0 = r * PER * M * DK
                        dve.tensor_tensor(on[:, c0:c0 + k * M * DK].rearrange("p (m i d) -> p m i d", m=M, i=k),
                                          cols[:, :, 0:DK * k].rearrange("p m (i d) -> p m i d", i=k),
                                          rec[:, :, 0:k].unsqueeze(3).broadcast_to([P, M, k, DK]),
                                          ALU.mult).then_inc(job_done, 1)
                    if j[0] == "oT":
                        low(j, oTL[:, :, :], ps.rearrange("p (k t) -> p k t", k=KB), oTH[:, :, :]
                            ).then_inc(job_done, 1)
                    if j[0] == "out":
                        b = j[1]
                        dve.wait_ge(job_ready, n + 1)
                        dve.wait_ge(bo_in, 16)
                        dve.wait_ge(xres_in, 16 * (b + 1))
                        dve.tensor_tensor(xres[:, :], xres[:, :], bob[:, :], ALU.add).then_inc(resid, 1)
                        dve.wait_ge(resid, b + 1)
                        since(dve, x1_written, 16 * b)
                        dve.tensor_tensor(x1[:, :], ps, xres[:, :], ALU.add).then_inc(job_done, 1)
                b, h = divmod(g, H)
                if 0 <= b < B and h in (HALF - 1, H - 1):
                    k = 2 * b + h // HALF
                    mine = mx[:, :, h + 1 - HALF:h + 1]
                    dve.wait_ge(max_ready, g + 1)
                    if k:
                        dve.wait_ge(job_ready, JOB["shift", (k - 1) // 2, (k - 1) % 2] + 1)
                    dve.tensor_copy(nm[:, :, 0, :], mine).then_inc(nm_ready, 1)
                    dve.wait_ge(nm_ready, 2 * k + 1)
                    dve.tensor_tensor(nm[:, :, 1, :], mine, nm[:, :, 0, :].bitcast(F32), ALU.subtract
                                      ).then_inc(nm_ready, 1)
            for b in range(B):
                dve.wait_ge(x1_in[b % 2], 16 * (b // 2 + 1))
                dve.bn_stats(stats2[:, :], x1in[b % 2][:, :]).then_inc(stat2, 1)
                dve.wait_ge(stat2, 3 * b + 1)
                dve.bn_aggr(mv2[:, :], stats2[:, :]).then_inc(stat2, 1)
                dve.wait_ge(stat2, 3 * b + 2)
                dve.tensor_scalar(ve2[:, :], mv2[:, 1:2], EPS, None, ALU.add).then_inc(stat2, 1)
                dve.wait_ge(rstd2_ready, b + 1)
                since(dve, x2T_ready, b)
                dve.tensor_scalar(x2n[:, :], x1in[b % 2][:, :], mv2[:, 0:1], rstd2[:, 0:1],
                                  ALU.subtract, ALU.mult).then_inc(x2n_ready, 1)
                dve.wait_ge(x2H_ready, b + 1)
                dve.tensor_tensor(x2L[:, :, b * S:b * S + S], PS[:, b % 4, :].rearrange("p (k t) -> p k t", k=KB),
                                  x2H[:, :, b * S:b * S + S].bitcast(F32), ALU.subtract).then_inc(x2L_ready, 1)
            for n in range(2 * FB):
                j = n % FB
                mj = min(P, F - j * P)
                if n < FB:
                    dve.wait_ge(ffw_high, 3 * (j + 1))
                    for t, (WL_, WH_) in enumerate(((gL, gH), (uL, uH))):
                        dve.tensor_tensor(WL_[:, :, j * P:j * P + mj],
                                          fin[t][:, 0:KB * mj].rearrange("p (k f) -> p k f", k=KB),
                                          WH_[:, :, j * P:j * P + mj].bitcast(F32), ALU.subtract
                                          ).then_inc(ffw_low, 1)
                    dve.tensor_tensor(dL[0:mj, j, :], fin[2][0:mj, :], dH[0:mj, j, :].bitcast(F32), ALU.subtract
                                      ).then_inc(ffw_low, 1)
                dve.wait_ge(th_ready, n + 1)
                dve.scalar_tensor_tensor(out=hu[0:mj, :], in0=th[0:mj, :], scalar=1.0, in1=PS[0:mj, 4 + n % 2, :],
                                         op0=ALU.add, op1=ALU.mult).then_inc(hu_ready, 1)
                dve.wait_ge(hu_ready, n + 1)
                dve.wait_ge(u_ready, n + 1)
                since(dve, hL_ready, n)
                dve.scalar_tensor_tensor(out=hf[0:mj, :], in0=hu[0:mj, :], scalar=0.5, in1=PS[0:mj, 6 + n % 2, :],
                                         op0=ALU.mult, op1=ALU.mult).then_inc(hf_ready, 1)
                dve.wait_ge(hH_ready, n + 1)
                dve.tensor_tensor(hL[n % 2][0:mj, :], hf[0:mj, :], hH[n % 2][0:mj, :].bitcast(F32), ALU.subtract
                                  ).then_inc(hL_ready, 1)
                if n == FB or n == 2 * FB - 1:
                    half = 0 if n == FB else 1
                    dve.wait_ge(y_ready, FB * (half + 1))
                    for t in range(4):
                        b = 4 * half + t
                        dve.wait_ge(x1_in[b % 2], 16 * (B // 2 + b // 2 + 1))
                        if b >= 2:
                            dve.wait_ge(out_written[b % 2], 16 * (b // 2))
                        dve.tensor_tensor(yo[b % 2][:, :], PS[:, t, :], x1in[b % 2][:, :], ALU.add
                                          ).then_inc(y_added, 1)

        @block.tensor
        def _(pe):
            def product(out_, lhs, rhs, n, stop=True):
                k = 0
                for i in range(n):
                    for l, r in ((0, 0), (0, 1), (1, 0)):
                        last = pe.matmul(out_, lhs(l, i), rhs(r, i), start=(k == 0), stop=(k == 3 * n - 1))
                        k += 1
                return last

            for g in steps:
                if 0 <= g < B * H:
                    b, h = divmod(g, H)
                    if h == 0:
                        pe.wait_ge(stack_in[QW][b % 2], 16 * (b // 2 + 1))
                    if h % GH == 0:
                        pe.wait_ge(bd_built[KW], M * (g // GH + 1))
                    since(pe, max_ready, g - 1)
                    pe.matmul(PS[:, g % 2, :], Qst[b % 2][:, h, :],
                              Kbd[g // GH % 2][:, h % GH].rearrange("p m t -> p (m t)"),
                              start=True, stop=True).then_inc(a_ready, 1)
                for j in at.get(g, []):
                    n = JOB.get(j)
                    if n is None:
                        continue
                    ps = PS[:, 6 + n % 2, :]
                    since(pe, job_done, n - 1)
                    if j[0] == "W":
                        _, w, k = j
                        pe.wait_ge(w_in[w], 16)
                        pe.wait_ge(mixed, 1 + 2 * KB)
                        for f in range(KB):
                            last = pe.matmul(ps[:, f * P:f * P + P], Wn[w][:, f, k * P:k * P + P], BD[:, f, :],
                                             start=True, stop=True)
                    if j[0] == "bias":
                        pe.wait_ge(wide, 1)
                        for f in range(KB):
                            last = pe.matmul(ps[:, f * P:f * P + P], bwide[:, j[1], f, :], BD[:, f, :],
                                             start=True, stop=True)
                    if j[0] == "proj":
                        _, w, b = j
                        if w == QW:
                            pe.wait_ge(job_done, JOB["xT", b] + 1)
                            X = (xTH, xTL)
                        else:
                            pe.wait_ge(low_ctx, b + 1)
                            X = (cH, cL)
                        last = product(ps, lambda p, i: X[p][:, i, :], lambda p, i: (WH, WL)[p][w][:, i, :], KB)
                    if j[0] == "xT":
                        pe.wait_ge(xn_ready, j[1] + 1)
                        for k in range(KB):
                            last = pe.transpose(ps[:, k * S:k * S + S], xin[:, k * P:k * P + P], ident[:, :])
                    if j[0] == "stack":
                        w = j[1]
                        pe.wait_ge(job_done, JOB["proj", w, j[2]] + 1)
                        for k in range(KB):
                            last = pe.transpose(ps[:, k * S:k * S + S], kq[w][:, k * P:k * P + P], ident[:, :])
                    if j[0] == "shift":
                        pe.wait_ge(nm_ready, 2 * (2 * j[1] + j[2]) + 2)
                        last = pe.transpose(ps[0:64, 0:S], nm[:, :, :, :].rearrange("p m s h -> p (m s h)").bitcast(F32),
                                            ident[:, :])
                    if j[0] == "norm_out":
                        rg = REG * j[1] + j[2]
                        pe.wait_ge(reg_ready, rg + 1)
                        last = pe.transpose(ps[:, 0:P], reg[rg % 2][:, :], ident[:, :])
                    if j[0] == "oT":
                        pe.wait_ge(job_done, JOB["norm_out", j[1], REG - 1] + 1)
                        for k in range(KB):
                            last = pe.transpose(ps[:, k * S:k * S + S], on[:, k * P:k * P + P], ident[:, :])
                    if j[0] == "out":
                        pe.wait_ge(job_done, JOB["oT", j[1]] + 1)
                        pe.wait_ge(wide, 2)
                        last = product(ps, lambda p, i: (oTH, oTL)[p][:, i, :],
                                       lambda p, i: (WH, WL)[p][3][:, i, :], KB)
                    last.then_inc(job_ready, 1)
                e = g - LAG_B
                if 0 <= e < B * H:
                    b, h = divmod(e, H)
                    if h % GH == 0:
                        pe.wait_ge(bd_built[QW], M * (e // GH + 1))
                    if h % HALF == 0:
                        pe.wait_ge(job_done, JOB["shift", b, h // HALF] + 1)
                    since(pe, exp_ready, e - 1)
                    pe.matmul(PS[:, 2 + e % 2, :], Kst[b % 2][:, h, :],
                              Qbd[e // GH % 2][:, h % GH].rearrange("p m t -> p (m t)"), start=True, stop=False)
                    pe.matmul(PS[:, 2 + e % 2, :], sel[:, h % HALF, :],
                              nmbd[e // HALF % 2][:, :, :].rearrange("p m t -> p (m t)"),
                              start=False, stop=True).then_inc(b_ready, 1)
                v = g - LAG_V
                if 0 <= v < B * H:
                    b, h = divmod(v, H)
                    r, i = divmod(h, PER)
                    rg = REG * b + r
                    if h == 0:
                        pe.wait_ge(job_done, JOB["proj", VW, b] + 1)
                    if i == 0:
                        since(pe, reg_ready, rg - 1)
                    pe.wait_ge(exp_ready, v + 1)
                    for m in range(M):
                        last = pe.matmul(PS[32 * m:32 * m + 32, 4 + rg % 2, 0:S], Vpad[b % 2][:, h, m, :],
                                         PT[v % PTN][:, m, :], start=(i == 0), stop=(h == region_last(r)),
                                         tile_position=(0, 32 * m))
                    last.then_inc(v_ready, 1)
            for b in range(B):
                pe.wait_ge(x2n_ready, b + 1)
                since(pe, x2L_ready, b - 3)
                for k in range(KB):
                    last = pe.transpose(PS[:, b % 4, k * S:k * S + S], x2n[:, k * P:k * P + P], ident[:, :])
                last.then_inc(x2T_ready, 1)

            def down(n):
                half, j = divmod(n, FB)
                mj = min(P, F - j * P)
                pe.wait_ge(hL_ready, n + 1)
                if j == 0 and half:
                    pe.wait_ge(y_added, 4)
                for t in range(4):
                    for k, (a, c) in enumerate(((hH, dH), (hH, dL), (hL, dH))):
                        last = pe.matmul(PS[:, t, :], a[n % 2][0:mj, t * S:t * S + S], c[0:mj, j, :],
                                         start=(j == 0 and k == 0), stop=(j == FB - 1 and k == 2))
                last.then_inc(y_ready, 1)

            for n in range(2 * FB):
                half, j = divmod(n, FB)
                mj = min(P, F - j * P)
                if n == 0:
                    pe.wait_ge(x2L_ready, B)
                pe.wait_ge(ffw_low, 3 * (j + 1))
                since(pe, hf_ready, n - 1)
                for W, bank, s in (((gH, gL), 4, g_ready), ((uH, uL), 6, u_ready)):
                    product(PS[0:mj, bank + n % 2, :], lambda p, i: W[p][:, i, j * P:j * P + mj],
                            lambda p, i: (x2H, x2L)[p][:, i, half * TOK:half * TOK + TOK], KB).then_inc(s, 1)
                if n >= 1:
                    down(n - 1)
            down(2 * FB - 1)


_OUTS = [((B, S, D), "float32")]


def kernel(**inputs):
    import numpy as _np
    import concourse.bacc as _bacc
    from concourse import mybir as _mybir
    from concourse.bass_utils import run_bass_kernel_spmd as _run

    a = {k: _np.asarray(v) for k, v in inputs.items()}
    rows = [h * M * DK + d * M + m
            for r in range(REG) for m in range(M) for h in range(PER * r, min(PER * r + PER, H)) for d in range(DK)]
    column = lambda v: v.reshape(KB, P).T
    laid = {
        "x": a["x"],
        "ctxT": a["ctx_4096"].transpose(0, 2, 1),
        "Wq": a["L0_xattn_Wq"], "Wk": a["L0_xattn_Wk"], "Wv": a["L0_xattn_Wv"],
        "WoT": a["L0_xattn_Wo"].T[rows],
        "bq": column(a["L0_xattn_bq"]), "bk": column(a["L0_xattn_bk"]), "bv": column(a["L0_xattn_bv"]),
        "bo": _np.broadcast_to(a["L0_xattn_bo"], (P, D)),
        "mix": _np.broadcast_to(a["L0_xattn_interference"][:, None], (H, DK, M, M)).reshape(H * DK * M, M),
        "amp": _np.broadcast_to(a["L0_xattn_amp"], (P, 1)),
        "WgT": a["L0_ffn_W_gate"].T, "WuT": a["L0_ffn_W_up"].T, "WdT": a["L0_ffn_W_down"].T,
    }
    nc = _bacc.Bacc("TRN2", target_bir_lowering=False, num_devices=1)
    arrays, args = {}, {}
    for name, v in laid.items():
        v = _np.ascontiguousarray(v)
        arrays[f"in_{name}_dram"] = v
        args[name] = nc.dram_tensor(f"in_{name}_dram", v.shape, _mybir.dt.from_np(v.dtype), kind="ExternalInput").ap()
    for i, (shape, dtype) in enumerate(_OUTS):
        args["out"] = nc.dram_tensor(f"out_{i}_dram", shape, _mybir.dt.from_np(_np.dtype(dtype)),
                                     kind="ExternalOutput").ap()
    build(nc, **args)
    r = _run(nc, [arrays], core_ids=[0])
    return r.results[0]["out_0_dram"]
```

```python
import concourse.bass as bass
from concourse import mybir
from contextlib import ExitStack

F32 = mybir.dt.float32
F32R = mybir.dt.float32r
ACT = mybir.ActivationFunctionType
ALU = mybir.AluOpType
AX = mybir.AxisListType

P = 128
B, S, D = 8, 128, 512
H, M, DK = 16, 4, 8
KB = D // P
GH = H // KB
F = 1376
FB = -(-F // P)
EPS = 1e-5
PARTS = 3
ROWS = M * PARTS * DK
PER = 3
REG = -(-H // PER)
LAG_B = 12
LAG_V = LAG_B + 2
HALF = H // 2
KST = 3
PTN = 3
TOK = 512
KW, QW, VW = range(3)
RC = 4
FIRST = -17
EARLY = 3


def region_last(r):
    return min(PER * r + PER, H) - 1


def plan():
    at = {}

    def place(step, *job):
        at.setdefault(max(step, FIRST), []).append(job)

    for w in (KW, QW, VW):
        for k in range(KB):
            place(FIRST, "W", w, k)
        place(FIRST, "bias", w)
    place(FIRST, "Wo")
    place(-10, "biasT")
    place(-9, "bias_out")
    for b in range(B):
        t = H * (b - 1)
        place(t - 3, "norm", b)
        place(t, "split_ctx", b)
        place(t + 1, "proj", KW, b)
        place(t + 3, "xT", b)
        place(t + 4, "stack", KW, b)
        place(t + 6, "proj", QW, b)
        place(t + 8, "stack", QW, b)
        place(t + 15, "proj", VW, b)
        t += H
        place(t + HALF + 1, "shift", b, 0)
        place(t + H + 1, "shift", b, 1)
        for c in range(2):
            place(t + region_last((RC, REG)[c] - 1) + LAG_V + 2, "norm_out", b, c)
        place(t + 33, "oT", b)
        place(t + 35, "out", b)
        place(t + 37, "norm2", b)
        place(t + 38, "x2T", b)
    for j in range(EARLY):
        place(H * (B - 1) + 2 + 4 * j, "ffw", j)
    place(H * B + LAG_B, "x2_load", 0)
    return range(FIRST, max(at) + 1), at


def build(nc, x, ctxT, Wq, Wk, Wv, WoT, bq, bk, bv, bo, mix, amp, WgT, WuT, WdT, out):
    steps, at = plan()
    NO_PRODUCT = ("split_ctx", "norm", "norm2", "Wo", "ffw", "x2_load")
    order = [j for g in steps for j in at.get(g, []) if j[0] not in NO_PRODUCT]
    JOB = {j: n for n, j in enumerate(order)}
    ON_ACT = ("W", "Wo", "xT", "stack", "oT", "x2T", "split_ctx", "shift", "biasT")
    every = [j for g in steps for j in at.get(g, [])]
    ACTED = {j: n + 1 for n, j in enumerate(j for j in every if j[0] in ON_ACT or j[:2] == ("proj", VW))}
    DONE = {j: n + 1 for n, j in enumerate(
        j for j in order if j[0] not in ("shift", "biasT", "norm_out") and j[:2] != ("proj", VW))}

    with ExitStack() as ctx:
        sem = lambda n: ctx.enter_context(nc.semaphore(n))
        scr = nc.dram_tensor("stack_scratch", [2, 2, M, PARTS, DK, H, S], F32, kind="Internal").ap()
        x2d = nc.dram_tensor("x2_scratch", [2, P, KB, B * S], F32, kind="Internal").ap()
        x1d = nc.dram_tensor("x1_scratch", [B, S, D], F32, kind="Internal").ap()
        PS = ctx.enter_context(nc.psum_tensor("PS", [P, 8, 512], F32))

        def alloc(stack):
            return lambda n, s, d=F32: stack.enter_context(nc.sbuf_tensor(n, s, d))

        sb = alloc(ctx)
        ident = sb("ident", [P, P])
        neghalf = sb("neghalf", [P, 1])

        one = ExitStack()
        sb = alloc(one)
        WH, WL = [None] * 4, [None] * 4
        for w in range(3):
            WH[w], WL[w] = sb(f"WH{w}", [P, KB, D], F32R), sb(f"WL{w}", [P, KB, D], F32R)
        prep = ExitStack()
        sbp = alloc(prep)
        Wn = [None] * 4
        for w in (3, 0, 1, 2):
            Wn[w] = sbp(f"Wn{w}", [P, KB, D])
        mixs = sbp("mixs", [P, KB, M])
        amps = sbp("amps", [P, 1])
        BD = sbp("BD", [P, KB, P])
        bcol = sbp("bcol", [P, 3, KB])
        bwide = sbp("bwide", [P, 3, KB, P])
        blk = sbp("blk", [P, P // M])
        selc = sbp("selc", [64, HALF])
        bvo = sbp("bvo", [P, D])
        bvT = sbp("bvT", [P, KB, P])
        prep.close()
        Kbd = [sb(f"Kbd{i}", [ROWS, GH, M, S], F32R) for i in range(2)]
        Qbd = [sb(f"Qbd{i}", [ROWS, GH, M, S], F32R) for i in range(2)]
        Kst = [sb(f"Kst{i}", [ROWS, H, S], F32R) for i in range(KST)]
        Qst = [sb(f"Qst{i}", [ROWS, H, S], F32R) for i in range(2)]
        WH[3], WL[3] = sb("WH3", [P, KB, D], F32R), sb("WL3", [P, KB, D], F32R)
        bias = [sb(f"bias{w}", [P, D]) for w in range(2)]
        bob = sb("bob", [P, D])
        mask96 = sb("mask96", [ROWS, M])
        mask64 = sb("mask64", [64, M])
        sel = sb("sel", [64, HALF, P], F32R)
        Vpad = [sb(f"Vpad{i}", [P, H, M, 32]) for i in range(2)]
        xin = sb("xin", [P, D])
        xres = sb("xres", [P, D])
        cin = sb("cin", [P, KB, S])
        cH = sb("cH", [P, KB, S], F32R)
        cL = sb("cL", [P, KB, S], F32R)
        stats = sb("stats", [P, 6])
        mv = sb("mv", [P, 2])
        ve = sb("ve", [P, 1])
        rstd = sb("rstd", [P, 1])
        xTH = sb("xTH", [P, KB, S], F32R)
        xTL = sb("xTL", [P, KB, S], F32R)
        kq = sb("kq", [P, D])
        kqH = [sb(f"kqH{w}", [P, M, S], F32R) for w in range(2)]
        kqL = [sb(f"kqL{w}", [P, M, S], F32R) for w in range(2)]
        mx = sb("mx", [P, M, H])
        nm = sb("nm", [P, M, 2, HALF], F32R)
        nmbd = [sb(f"nmbd{i}", [64, M, S], F32R) for i in range(2)]
        PT = [sb(f"PT{i}", [P, M, S]) for i in range(PTN)]
        reg = [sb(f"reg{i}", [P, S]) for i in range(REG)]
        rec = sb("rec", [P, RC * M, PER])
        on = sb("on", [P, D])
        oTH = sb("oTH", [P, KB, S], F32R)
        oTL = sb("oTL", [P, KB, S], F32R)
        stats2 = sb("stats2", [P, 6])
        mv2 = sb("mv2", [P, 2])
        ve2 = sb("ve2", [P, 1])
        rstd2 = sb("rstd2", [P, 1])
        one.close()

        two = ExitStack()
        sb = alloc(two)
        fin = [[sb(f"fin{i}{k}", [P, D]) for k in range(3)] for i in range(2)]
        gH, gL, uH, uL, dH, dL = fw = [[] for _ in range(6)]

        def block_of_weights(j):
            for k, name in enumerate(("gH", "gL", "uH", "uL", "dH", "dL")):
                fw[k].append(sb(f"{name}{j}", [P, D], F32R))

        for j in range(EARLY):
            block_of_weights(j)
        x2 = [[sb(f"x2{p}{i}", [P, KB, TOK], F32R) for p in "HL"] for i in range(2)]
        for j in range(EARLY, FB):
            block_of_weights(j)
        x1in = [sb(f"x1in{i}", [P, D]) for i in range(2)]
        th = sb("th", [P, TOK])
        hu = sb("hu", [P, TOK])
        hf = sb("hf", [P, TOK])
        hH = [sb(f"hH{i}", [P, TOK], F32R) for i in range(2)]
        hL = [sb(f"hL{i}", [P, TOK], F32R) for i in range(2)]
        yo = [sb(f"yo{i}", [P, D]) for i in range(2)]
        two.close()

        mix_in, bias_in, bo_in = [sem(n) for n in ("mix_in", "bias_in", "bo_in")]
        w_in = [sem(f"w_in{w}") for w in range(4)]
        x_in, c_in, xres_in = sem("x_in"), sem("c_in"), sem("xres_in")
        stack_written = [sem(f"stack_written{w}") for w in range(2)]
        stack_in = [[sem(f"stack_in{w}{i}") for i in range((KST, 2)[w])] for w in range(2)]
        x1_written = sem("x1_written")
        pool_setup, dve_setup, mixed, wide = sem("pool_setup"), sem("dve_setup"), sem("mixed"), sem("wide")
        job_ready, dve_done, act_done = sem("job_ready"), sem("dve_done"), sem("act_done")
        low_ctx, stat, rstd_ready, xn_ready = sem("low_ctx"), sem("stat"), sem("rstd_ready"), sem("xn_ready")
        nm_ready, rec_ready, on_ready, resid = sem("nm_ready"), sem("rec_ready"), sem("on_ready"), sem("resid")
        a_ready, max_ready, b_ready, exp_ready, v_ready, reg_ready = [
            sem(n) for n in ("a_ready", "max_ready", "b_ready", "exp_ready", "v_ready", "reg_ready")]
        bd_built = [sem("kbd_built"), sem("qbd_built")]
        x1_in = [sem(f"x1_in{i}") for i in range(2)]
        stat2, rstd2_ready, x2n_ready = [sem(n) for n in ("stat2", "rstd2_ready", "x2n_ready")]
        x2_written, x2_in = sem("x2_written"), [sem(f"x2_in{i}") for i in range(2)]
        ffw_in = [sem(f"ffw_in{i}") for i in range(2)]
        ffw_high, ffw_low = sem("ffw_high"), sem("ffw_low")
        g_ready, u_ready, th_ready, hu_ready, hf_ready, hH_ready, hL_ready, y_ready = [
            sem(n) for n in ("g_ready", "u_ready", "th_ready", "hu_ready", "hf_ready", "hH_ready", "hL_ready", "y_ready")]
        y_added = sem("y_added")
        out_written = [sem(f"out_written{i}") for i in range(2)]

        def since(eng, s, n):
            if n > 0:
                eng.wait_ge(s, n)

        def ended(eng, *j):
            if j[0] == "norm_out":
                eng.wait_ge(on_ready, 3 * j[1] + 1 + 2 * j[2])
            elif j in DONE:
                eng.wait_ge(dve_done, DONE[j])
            else:
                eng.wait_ge(act_done, ACTED[j])

        def multiplied(eng, *j):
            eng.wait_ge(job_ready, JOB[j] + 1)

        block = ctx.enter_context(nc.Block())

        @block.sync
        def _(sp):
            sp.dma_start(mixs[:, :, :], mix.rearrange("(g p) j -> p g j", p=P)).then_inc(mix_in, 16)
            sp.dma_start(amps[:, :], amp).then_inc(mix_in, 16)
            for w, (W, bb) in enumerate(((Wk, bk), (Wq, bq), (Wv, bv))):
                sp.dma_start(Wn[w][:, :, :], W.rearrange("(g p) c -> p g c", p=P)).then_inc(w_in[w], 16)
                sp.dma_start(bcol[:, w, :], bb).then_inc(bias_in, 16)
            sp.dma_start(Wn[3][:, :, :], WoT.rearrange("(k p) n -> p k n", p=P)).then_inc(w_in[3], 16)
            sp.dma_start(bob[:, :], bo).then_inc(bo_in, 16)

            def load_weights(j):
                mj = min(P, F - j * P)
                since(sp, ffw_low, 3 * (j - 1))
                for t, W in enumerate((WgT, WuT)):
                    sp.dma_start(fin[j % 2][t][:, 0:KB * mj].rearrange("p (k f) -> p k f", k=KB),
                                 W[:, j * P:j * P + mj].rearrange("(k p) f -> p k f", p=P)).then_inc(ffw_in[j % 2], 16)
                sp.dma_start(fin[j % 2][2][0:mj, :], WdT[j * P:j * P + mj, :]).then_inc(ffw_in[j % 2], 16)

            def load_x2(half):
                for p in range(2):
                    sp.dma_start(x2[half][p][:, :, :].bitcast(F32), x2d[p, :, :, half * TOK:half * TOK + TOK]
                                 ).then_inc(x2_in[half], 16)

            for g in steps:
                for j in at.get(g, []):
                    b = j[-1]
                    if j[0] == "split_ctx":
                        since(sp, low_ctx, b)
                        sp.dma_start(cin[:, :, :], ctxT[b].rearrange("(k p) t -> p k t", p=P)).then_inc(c_in, 16)
                    if j[0] == "norm" and b == 0:
                        sp.dma_start(xin[:, :], x[b]).then_inc(x_in, 16)
                    if j[0] == "xT" and b + 1 < B:
                        multiplied(sp, *j)
                        sp.dma_start(xin[:, :], x[b + 1]).then_inc(x_in, 16)
                    if j[0] == "stack":
                        w = j[1]
                        ended(sp, *j)
                        own = scr[w, b % 2]
                        for part, src in enumerate(((kqH, kqL, kqH), (kqH, kqH, kqL))[w]):
                            sp.dma_start(own[:, part].rearrange("m d h t -> (d h) m t"),
                                         src[w][:, :, :].bitcast(F32)).then_inc(stack_written[w], 16)
                        sp.wait_ge(stack_written[w], 16 * PARTS * (b + 1))
                        ring = (KST, 2)[w]
                        if b == 0:
                            ended(sp, "bias_out")
                        if b >= ring:
                            sp.wait_ge((b_ready, a_ready)[w], H * (b - ring + 1))
                            sp.wait_ge(bd_built[w], M * KB * (b - ring + 1))
                        sp.dma_start((Kst, Qst)[w][b % ring][:, :, :].rearrange("p h t -> p (h t)").bitcast(F32),
                                     own.rearrange("m s d h t -> (m s d) (h t)")).then_inc(stack_in[w][b % ring], 16)
                    if j[0] == "oT":
                        since(sp, x2n_ready, b)
                        since(sp, x1_written, 16 * b)
                        sp.dma_start(xres[:, :], x[b]).then_inc(xres_in, 16)
                    if j[0] == "out":
                        ended(sp, *j)
                        sp.dma_start(x1d[b], xres[:, :]).then_inc(x1_written, 16)
                    if j[0] == "x2T":
                        ended(sp, *j)
                        for p, src in enumerate((oTH, oTL)):
                            sp.dma_start(x2d[p, :, :, b * S:b * S + S], src[:, :, :].bitcast(F32)
                                         ).then_inc(x2_written, 16)
                    if j[0] == "ffw":
                        if b == 0:
                            ended(sp, "proj", VW, B - 1)
                        load_weights(b)
                    if j[0] == "x2_load":
                        sp.wait_ge(a_ready, B * H)
                        sp.wait_ge(x2_written, 32 * 4)
                        load_x2(0)
            sp.wait_ge(x2_written, 32 * B)
            sp.wait_ge(b_ready, B * H)
            load_x2(1)
            sp.wait_ge(x1_written, 16 * B)
            for j in range(EARLY, FB):
                load_weights(j)
            for b in range(B):
                if b >= 2:
                    sp.wait_ge(y_added, b - 1)
                sp.dma_start(x1in[b % 2][:, :], x1d[b]).then_inc(x1_in[b % 2], 16)
                if b >= 1:
                    sp.wait_ge(y_added, b)
                    sp.dma_start(out[b - 1], yo[(b - 1) % 2][:, :]).then_inc(out_written[(b - 1) % 2], 16)
            sp.wait_ge(y_added, B)
            sp.dma_start(out[B - 1], yo[(B - 1) % 2][:, :]).then_inc(out_written[(B - 1) % 2], 16)
            for written in out_written:
                sp.wait_ge(written, 16 * (B // 2))

        @block.gpsimd
        def _(pool):
            pool.memset(ident[:, :], 0.0).then_inc(pool_setup, 1)
            pool.memset(neghalf[:, :], -0.5).then_inc(pool_setup, 1)
            pool.wait_ge(pool_setup, 2)
            pool.affine_select(out=ident[:, :], in_=ident[:, :], compare_op=ALU.not_equal, fill=1.0, base=0,
                               pattern=[[-1, P]], channel_multiplier=1).then_inc(pool_setup, 1)
            for v in Vpad:
                pool.memset(v[:, :, :, :], 0.0).then_inc(pool_setup, 1)
            pool.wait_ge(pool_setup, 5)
            for v in Vpad:
                for i in range(PER):
                    pool.memset(v[:, i:H:PER, :, DK * PER + i], 1.0).then_inc(pool_setup, 1)

            def spread(w, q):
                b, u = q // KB, q % KB
                ring = (KST, 2)[w]
                pool.wait_ge(stack_in[w][b % ring], 16 * (b // ring + 1))
                since(pool, (a_ready, b_ready)[w], GH * (q - 1))
                st, bd = ((Kst, Kbd), (Qst, Qbd))[w]
                for m in range(M):
                    pool.tensor_scalar(bd[q % 2][:, :, m, :], st[b % ring][:, GH * u:GH * u + GH, :].bitcast(F32),
                                       mask96[:, m:m + 1], 1.0, ALU.mult, ALU.mult).then_inc(bd_built[w], 1)

            def power(b):
                pool.wait_ge(stat, 3 * b + 3)
                pool.tensor_tensor(rstd[:, :], ve[:, :], neghalf[:, :], ALU.pow).then_inc(rstd_ready, 1)

            def power2(b):
                pool.wait_ge(stat2, 3 * b + 3)
                pool.tensor_tensor(rstd2[:, :], ve2[:, :], neghalf[:, :], ALU.pow).then_inc(rstd2_ready, 1)

            pool.wait_ge(dve_setup, 1)
            power(0)
            spread(KW, 0)
            for q in range(KB * (B + 2) + 2):
                b, u = divmod(q, KB)
                if u == 0 and 0 < b + 1 < B:
                    power(b + 1)
                if u == 1 and 0 <= b - 2 < B:
                    power2(b - 2)
                if 0 <= q - 2 < KB * B:
                    spread(QW, q - 2)
                if q + 1 < KB * B:
                    spread(KW, q + 1)

        @block.scalar
        def _(act):
            def high(dst, src):
                act.activation(dst, src, ACT.Copy).then_inc(act_done, 1)

            def split_h_high(n):
                mj = min(P, F - (n % FB) * P)
                act.wait_ge(hf_ready, n + 1)
                since(act, y_ready, n - 1)
                act.activation(hH[n % 2][0:mj, :], hf[0:mj, :], ACT.Copy).then_inc(hH_ready, 1)

            def split_weights_high(j):
                mj = min(P, F - j * P)
                act.wait_ge(ffw_in[j % 2], 48 * (j // 2 + 1))
                for t, W in enumerate((gH, uH)):
                    act.activation(W[j][:, 0:KB * mj], fin[j % 2][t][:, 0:KB * mj], ACT.Copy).then_inc(ffw_high, 1)
                act.activation(dH[j][0:mj, :], fin[j % 2][2][0:mj, :], ACT.Copy).then_inc(ffw_high, 1)

            for g in steps:
                for j in at.get(g, []):
                    b = j[-1]
                    n = JOB.get(j)
                    ps = None if n is None else PS[:, 6 + n % 2, :]
                    if j[0] == "W":
                        _, w, k = j
                        multiplied(act, *j)
                        high(WH[w][:, k, :].rearrange("p (m d h) -> p m d h", m=M, d=DK),
                             ps.rearrange("p (h d m) -> p m d h", h=H, d=DK))
                    if j[0] == "Wo":
                        act.wait_ge(w_in[3], 16)
                        high(WH[3][:, :, :], Wn[3][:, :, :])
                    if j[0] == "biasT":
                        multiplied(act, *j)
                        high(bvT[:, :, :], ps.rearrange("p (k t) -> p k t", k=KB))
                    if j[0] == "split_ctx":
                        act.wait_ge(c_in, 16 * (b + 1))
                        if b:
                            multiplied(act, "proj", VW, b - 1)
                        high(cH[:, :, :], cin[:, :, :])
                    if j[0] == "xT":
                        multiplied(act, *j)
                        high(xTH[:, :, :], ps.rearrange("p (k t) -> p k t", k=KB))
                    if j[0] == "stack":
                        w = j[1]
                        multiplied(act, *j)
                        since(act, stack_written[w], 16 * PARTS * b)
                        high(kqH[w][:, :, :], ps.rearrange("p (m t) -> p m t", m=M))
                    if j[:2] == ("proj", VW):
                        multiplied(act, *j)
                        act.wait_ge(pool_setup, 11)
                        since(act, v_ready, H * (b - 1))
                        for i in range(PER):
                            last = act.activation(Vpad[b % 2][:, i:H:PER, :, DK * i:DK * i + DK],
                                                  ps.rearrange("p (m d h) -> p h m d", m=M, d=DK)[:, i:H:PER],
                                                  ACT.Copy)
                        last.then_inc(act_done, 1)
                    if j[0] == "shift":
                        _, b, half = j
                        k = 2 * b + half
                        multiplied(act, *j)
                        since(act, b_ready, HALF * (k - 1))
                        for m in range(M):
                            last = act.activation(nmbd[k % 2][:, m, :], ps[0:64, 0:S], ACT.Copy,
                                                  scale=mask64[:, m:m + 1])
                        last.then_inc(act_done, 1)
                    if j[0] == "oT":
                        multiplied(act, *j)
                        since(act, x2_written, 32 * b)
                        high(oTH[:, :, :], ps.rearrange("p (k t) -> p k t", k=KB))
                    if j[0] == "x2T":
                        multiplied(act, *j)
                        high(oTH[:, :, :], ps.rearrange("p (k t) -> p k t", k=KB))
                    if j[0] == "ffw":
                        if b == 0:
                            ended(act, "proj", VW, B - 1)
                        split_weights_high(b)
                e = g - LAG_B
                if 0 <= e < B * H:
                    act.wait_ge(b_ready, e + 1)
                    since(act, v_ready, e - PTN + 1)
                    act.activation(PT[e % PTN][:, :, :], PS[:, 2 + e % 2, :].rearrange("p (m t) -> p m t", m=M),
                                   ACT.Exp, scale=DK ** -0.5).then_inc(exp_ready, 1)
                b, h = divmod(g - LAG_V - 1, H)
                if 0 <= b < B and h in [region_last(r) for r in range(REG)]:
                    r = h // PER
                    act.wait_ge(v_ready, H * b + h + 1)
                    if b:
                        multiplied(act, "norm_out", b - 1, int(r >= RC))
                    act.activation(reg[r][:, :], PS[:, 4 + (REG * b + r) % 2, 0:S], ACT.Copy).then_inc(reg_ready, 1)
            for n in range(2 * FB):
                j = n % FB
                mj = min(P, F - j * P)
                if n == 0:
                    ended(act, "x2T", B - 1)
                    split_weights_high(EARLY)
                if n + EARLY + 1 < FB:
                    split_weights_high(n + EARLY + 1)
                if n >= 1:
                    split_h_high(n - 1)
                act.wait_ge(g_ready, n + 1)
                since(act, hu_ready, n)
                act.activation(th[0:mj, :], PS[0:mj, 4 + n % 2, :], ACT.Tanh, scale=0.5).then_inc(th_ready, 1)
            split_h_high(2 * FB - 1)

        @block.vector
        def _(dve):
            dve.wait_ge(pool_setup, 3)
            dve.tensor_reduce(mask96[:, :], ident[0:ROWS, 0:ROWS].rearrange("p (m j) -> p m j", m=M),
                              AX.X, ALU.add).then_inc(dve_setup, 1)
            dve.tensor_reduce(mask64[:, :], ident[0:64, 0:64].rearrange("p (m j) -> p m j", m=M),
                              AX.X, ALU.add).then_inc(dve_setup, 1)
            dve.tensor_reduce(selc[:, :], ident[0:64, 0:64].rearrange("p (j h) -> p h j", h=HALF),
                              AX.X, ALU.add).then_inc(dve_setup, 1)
            dve.tensor_reduce(blk[:, :], ident[:, :].rearrange("p (k j) -> p k j", j=M),
                              AX.X, ALU.add).then_inc(dve_setup, 1)
            dve.wait_ge(mix_in, 32)
            dve.tensor_scalar(mixs[:, :, :], mixs[:, :, :], amps[:, 0:1], 0.1, ALU.mult, ALU.mult).then_inc(mixed, 1)
            dve.wait_ge(mixed, 1)
            dve.wait_ge(dve_setup, 4)
            for g in range(KB):
                dve.tensor_tensor(BD[:, g, :].rearrange("p (k j) -> p k j", j=M),
                                  mixs[:, g, :].unsqueeze(1).broadcast_to([P, P // M, M]),
                                  blk[:, :].unsqueeze(2).broadcast_to([P, P // M, M]), ALU.mult).then_inc(mixed, 1)
            dve.wait_ge(mixed, 1 + KB)
            for g in range(KB):
                dve.tensor_tensor(BD[:, g, :], BD[:, g, :], ident[:, :], ALU.add).then_inc(mixed, 1)
            dve.tensor_copy(sel[:, :, :], selc[:, :].unsqueeze(2).broadcast_to([64, HALF, P])).then_inc(dve_setup, 1)
            dve.wait_ge(bias_in, 48)
            dve.tensor_copy(bwide[:, :, :, :].rearrange("p w g t -> p (w g) t"),
                            bcol[:, :, :].rearrange("p w g -> p (w g)").unsqueeze(2).broadcast_to([P, 3 * KB, P])
                            ).then_inc(wide, 1)

            def low(j, dst, src, hi):
                dve.wait_ge(act_done, ACTED[j])
                return dve.tensor_tensor(dst, src, hi.bitcast(F32), ALU.subtract)

            def split_weights_low(j):
                mj = min(P, F - j * P)
                for t, (lo, hi, rows, cols) in enumerate(
                        ((gL, gH, P, KB * mj), (uL, uH, P, KB * mj), (dL, dH, mj, D))):
                    dve.wait_ge(ffw_high, 3 * j + t + 1)
                    dve.tensor_tensor(lo[j][0:rows, 0:cols], fin[j % 2][t][0:rows, 0:cols],
                                      hi[j][0:rows, 0:cols].bitcast(F32), ALU.subtract).then_inc(ffw_low, 1)

            def moments(rows, arrived, count, st, m, v, done, b):
                dve.wait_ge(arrived, count)
                dve.bn_stats(st[:, :], rows[:, :]).then_inc(done, 1)
                dve.wait_ge(done, 3 * b + 1)
                dve.bn_aggr(m[:, :], st[:, :]).then_inc(done, 1)
                dve.wait_ge(done, 3 * b + 2)
                dve.tensor_scalar(v[:, :], m[:, 1:2], EPS, None, ALU.add).then_inc(done, 1)

            rec_used = [0]
            for g in steps:
                if 0 <= g < B * H:
                    b, h = divmod(g, H)
                    dve.wait_ge(a_ready, g + 1)
                    dve.tensor_reduce(mx[:, :, h], PS[:, g % 2, :].rearrange("p (m t) -> p m t", m=M),
                                      AX.X, ALU.max, negate=True).then_inc(max_ready, 1)
                for j in at.get(g, []):
                    b = j[-1]
                    n = JOB.get(j)
                    ps = None if n is None else PS[:, 6 + n % 2, :]
                    if j[0] == "W":
                        _, w, k = j
                        low(j, WL[w][:, k, :].rearrange("p (m d h) -> p m d h", m=M, d=DK),
                            ps.rearrange("p (h d m) -> p m d h", h=H, d=DK),
                            WH[w][:, k, :].rearrange("p (m d h) -> p m d h", m=M, d=DK)).then_inc(dve_done, 1)
                    if j[0] == "bias" and j[1] != VW:
                        multiplied(dve, *j)
                        dve.tensor_copy(bias[j[1]][:, :].rearrange("p (m d h) -> p m d h", m=M, d=DK),
                                        ps.rearrange("p (h d m) -> p m d h", h=H, d=DK)).then_inc(dve_done, 1)
                    if j == ("bias", VW):
                        multiplied(dve, *j)
                        for r in range(REG):
                            k = min(PER, H - PER * r)
                            c0 = r * PER * M * DK
                            last = dve.tensor_copy(
                                bvo[:, c0:c0 + k * M * DK].rearrange("p (m i d) -> p m i d", m=M, i=k),
                                ps[:, c0:c0 + k * M * DK].rearrange("p (i d m) -> p m i d", m=M, i=k))
                        last.then_inc(dve_done, 1)
                    if j[0] == "bias_out":
                        multiplied(dve, *j)
                        dve.wait_ge(bo_in, 16)
                        dve.tensor_tensor(bob[:, :], ps, bob[:, :], ALU.add).then_inc(dve_done, 1)
                    if j[0] == "Wo":
                        low(j, WL[3][:, :, :], Wn[3][:, :, :], WH[3][:, :, :]).then_inc(wide, 1)
                    if j[0] == "split_ctx":
                        low(j, cL[:, :, :], cin[:, :, :], cH[:, :, :]).then_inc(low_ctx, 1)
                    if j[0] == "norm":
                        moments(xin, x_in, 16 * (b + 1), stats, mv, ve, stat, b)
                    if j[:2] == ("proj", KW):
                        dve.wait_ge(rstd_ready, b + 1)
                        dve.tensor_scalar(xin[:, :], xin[:, :], mv[:, 0:1], rstd[:, 0:1],
                                          ALU.subtract, ALU.mult).then_inc(xn_ready, 1)
                    if j[0] == "proj" and j[1] != VW:
                        multiplied(dve, *j)
                        dve.tensor_tensor(kq[:, :], ps, bias[j[1]][:, :], ALU.add).then_inc(dve_done, 1)
                    if j[0] == "xT":
                        low(j, xTL[:, :, :], ps.rearrange("p (k t) -> p k t", k=KB), xTH[:, :, :]
                            ).then_inc(dve_done, 1)
                    if j[0] == "stack":
                        w = j[1]
                        low(j, kqL[w][:, :, :], ps.rearrange("p (m t) -> p m t", m=M), kqH[w][:, :, :]
                            ).then_inc(dve_done, 1)
                    if j[0] == "norm_out":
                        _, b, c = j
                        multiplied(dve, *j)
                        for r0, nr, k in (((0, RC, PER),), ((RC, REG - RC - 1, PER), (REG - 1, 1, H - PER * (REG - 1)))
                                          )[c]:
                            cols = ps[:, (r0 - RC * c) * P:(r0 - RC * c + nr) * P].rearrange("p (s c) -> p s c", c=32)
                            if rec_used[0]:
                                dve.wait_ge(on_ready, rec_used[0])
                            rec_used[0] += 1
                            sums = rec[:, 0:nr * M, 0:k]
                            dve.reciprocal(sums, cols[:, :, DK * PER:DK * PER + k]).then_inc(rec_ready, 1)
                            dve.wait_ge(rec_ready, rec_used[0])
                            c0 = r0 * PER * M * DK
                            dve.tensor_tensor(
                                on[:, c0:c0 + nr * k * M * DK].rearrange("p (s i d) -> p s i d", s=nr * M, i=k),
                                cols[:, :, 0:DK * k].rearrange("p s (i d) -> p s i d", i=k),
                                sums.unsqueeze(3).broadcast_to([P, nr * M, k, DK]), ALU.mult).then_inc(on_ready, 1)
                    if j[0] == "oT":
                        low(j, oTL[:, :, :], ps.rearrange("p (k t) -> p k t", k=KB), oTH[:, :, :]
                            ).then_inc(dve_done, 1)
                    if j[0] == "out":
                        dve.wait_ge(xres_in, 16 * (b + 1))
                        dve.tensor_tensor(xres[:, :], xres[:, :], bob[:, :], ALU.add).then_inc(resid, 1)
                        dve.wait_ge(resid, b + 1)
                        multiplied(dve, *j)
                        dve.tensor_tensor(xres[:, :], ps, xres[:, :], ALU.add).then_inc(dve_done, 1)
                        moments(xres, dve_done, DONE[j], stats2, mv2, ve2, stat2, b)
                    if j[0] == "norm2":
                        dve.wait_ge(rstd2_ready, b + 1)
                        if b:
                            multiplied(dve, "x2T", b - 1)
                        dve.tensor_scalar(on[:, :], xres[:, :], mv2[:, 0:1], rstd2[:, 0:1],
                                          ALU.subtract, ALU.mult).then_inc(x2n_ready, 1)
                    if j[0] == "x2T":
                        low(j, oTL[:, :, :], ps.rearrange("p (k t) -> p k t", k=KB), oTH[:, :, :]
                            ).then_inc(dve_done, 1)
                    if j[0] == "ffw":
                        split_weights_low(b)
                b, h = divmod(g, H)
                if 0 <= b < B and h in (HALF - 1, H - 1):
                    k = 2 * b + h // HALF
                    mine = mx[:, :, h + 1 - HALF:h + 1]
                    dve.wait_ge(max_ready, g + 1)
                    if k:
                        multiplied(dve, "shift", (k - 1) // 2, (k - 1) % 2)
                    dve.tensor_copy(nm[:, :, 0, :], mine).then_inc(nm_ready, 1)
                    dve.wait_ge(nm_ready, 2 * k + 1)
                    dve.tensor_tensor(nm[:, :, 1, :], mine, nm[:, :, 0, :].bitcast(F32), ALU.subtract
                                      ).then_inc(nm_ready, 1)
            for n in range(2 * FB):
                j = n % FB
                mj = min(P, F - j * P)
                if n == 0:
                    split_weights_low(EARLY)
                if n + EARLY + 1 < FB:
                    split_weights_low(n + EARLY + 1)
                dve.wait_ge(th_ready, n + 1)
                since(dve, hf_ready, n)
                dve.scalar_tensor_tensor(out=hu[0:mj, :], in0=th[0:mj, :], scalar=1.0, in1=PS[0:mj, 4 + n % 2, :],
                                         op0=ALU.add, op1=ALU.mult).then_inc(hu_ready, 1)
                dve.wait_ge(hu_ready, n + 1)
                dve.wait_ge(u_ready, n + 1)
                since(dve, hL_ready, n)
                dve.scalar_tensor_tensor(out=hf[0:mj, :], in0=hu[0:mj, :], scalar=0.5, in1=PS[0:mj, 6 + n % 2, :],
                                         op0=ALU.mult, op1=ALU.mult).then_inc(hf_ready, 1)
                dve.wait_ge(hH_ready, n + 1)
                dve.tensor_tensor(hL[n % 2][0:mj, :], hf[0:mj, :], hH[n % 2][0:mj, :].bitcast(F32), ALU.subtract
                                  ).then_inc(hL_ready, 1)
                if n == FB or n == 2 * FB - 1:
                    half = 0 if n == FB else 1
                    dve.wait_ge(y_ready, FB * (half + 1))
                    for t in range(4):
                        b = 4 * half + t
                        dve.wait_ge(x1_in[b % 2], 16 * (b // 2 + 1))
                        if b >= 2:
                            dve.wait_ge(out_written[b % 2], 16 * (b // 2))
                        dve.tensor_tensor(yo[b % 2][:, :], PS[:, t, :], x1in[b % 2][:, :], ALU.add
                                          ).then_inc(y_added, 1)

        @block.tensor
        def _(pe):
            def product(out_, lhs, rhs, n):
                k = 0
                for i in range(n):
                    for l, r in ((0, 0), (0, 1), (1, 0)):
                        last = pe.matmul(out_, lhs(l, i), rhs(r, i), start=(k == 0), stop=(k == 3 * n - 1))
                        k += 1
                return last

            for g in steps:
                if 0 <= g < B * H:
                    b, h = divmod(g, H)
                    if h == 0:
                        pe.wait_ge(stack_in[QW][b % 2], 16 * (b // 2 + 1))
                    if h % GH == 0:
                        pe.wait_ge(bd_built[KW], M * (g // GH + 1))
                    since(pe, max_ready, g - 1)
                    pe.matmul(PS[:, g % 2, :], Qst[b % 2][:, h, :],
                              Kbd[g // GH % 2][:, h % GH].rearrange("p m t -> p (m t)"),
                              start=True, stop=True).then_inc(a_ready, 1)
                for j in at.get(g, []):
                    b = j[-1]
                    n = JOB.get(j)
                    if n is None:
                        continue
                    ps = PS[:, 6 + n % 2, :]
                    if n >= 2:
                        ended(pe, *order[n - 2])
                    if j[0] == "W":
                        _, w, k = j
                        pe.wait_ge(w_in[w], 16)
                        pe.wait_ge(mixed, 1 + 2 * KB)
                        for f in range(KB):
                            last = pe.matmul(ps[:, f * P:f * P + P], Wn[w][:, f, k * P:k * P + P], BD[:, f, :],
                                             start=True, stop=True)
                    if j[0] == "bias":
                        pe.wait_ge(wide, 1)
                        for f in range(KB):
                            last = pe.matmul(ps[:, f * P:f * P + P], bwide[:, j[1], f, :], BD[:, f, :],
                                             start=True, stop=True)
                    if j[0] == "biasT":
                        ended(pe, "bias", VW)
                        for k in range(KB):
                            last = pe.transpose(ps[:, k * S:k * S + S], bvo[:, k * P:k * P + P], ident[:, :])
                    if j[0] == "bias_out":
                        ended(pe, "biasT")
                        pe.wait_ge(w_in[3], 16)
                        for k in range(KB):
                            last = pe.matmul(ps, bvT[:, k, :], Wn[3][:, k, :], start=(k == 0), stop=(k == KB - 1))
                    if j[0] == "proj":
                        w = j[1]
                        if w == QW:
                            ended(pe, "xT", b)
                            X = (xTH, xTL)
                        else:
                            pe.wait_ge(low_ctx, b + 1)
                            X = (cH, cL)
                        last = product(ps, lambda p, i: X[p][:, i, :], lambda p, i: (WH, WL)[p][w][:, i, :], KB)
                    if j[0] == "xT":
                        pe.wait_ge(xn_ready, b + 1)
                        for k in range(KB):
                            last = pe.transpose(ps[:, k * S:k * S + S], xin[:, k * P:k * P + P], ident[:, :])
                    if j[0] == "stack":
                        w = j[1]
                        ended(pe, "proj", w, b)
                        for k in range(KB):
                            last = pe.transpose(ps[:, k * S:k * S + S], kq[:, k * P:k * P + P], ident[:, :])
                    if j[0] == "shift":
                        pe.wait_ge(nm_ready, 2 * (2 * j[1] + j[2]) + 2)
                        last = pe.transpose(ps[0:64, 0:S], nm[:, :, :, :].rearrange("p m s h -> p (m s h)").bitcast(F32),
                                            ident[:, :])
                    if j[0] == "norm_out":
                        _, b, c = j
                        pe.wait_ge(reg_ready, REG * b + (RC, REG)[c])
                        for r in range(*((0, RC), (RC, REG))[c]):
                            last = pe.transpose(ps[:, (r - RC * c) * P:(r - RC * c + 1) * P], reg[r][:, :], ident[:, :])
                    if j[0] == "oT":
                        pe.wait_ge(on_ready, 3 * (b + 1))
                        for k in range(KB):
                            last = pe.transpose(ps[:, k * S:k * S + S], on[:, k * P:k * P + P], ident[:, :])
                    if j[0] == "x2T":
                        pe.wait_ge(x2n_ready, b + 1)
                        for k in range(KB):
                            last = pe.transpose(ps[:, k * S:k * S + S], on[:, k * P:k * P + P], ident[:, :])
                    if j[0] == "out":
                        ended(pe, "oT", b)
                        pe.wait_ge(wide, 2)
                        last = product(ps, lambda p, i: (oTH, oTL)[p][:, i, :],
                                       lambda p, i: (WH, WL)[p][3][:, i, :], KB)
                    last.then_inc(job_ready, 1)
                e = g - LAG_B
                if 0 <= e < B * H:
                    b, h = divmod(e, H)
                    if h == 0:
                        pe.wait_ge(stack_in[KW][b % KST], 16 * (b // KST + 1))
                    if h % GH == 0:
                        pe.wait_ge(bd_built[QW], M * (e // GH + 1))
                    if h % HALF == 0:
                        ended(pe, "shift", b, h // HALF)
                        pe.wait_ge(dve_setup, 5)
                    since(pe, exp_ready, e - 1)
                    pe.matmul(PS[:, 2 + e % 2, :], Kst[b % KST][:, h, :],
                              Qbd[e // GH % 2][:, h % GH].rearrange("p m t -> p (m t)"), start=True, stop=False)
                    pe.matmul(PS[:, 2 + e % 2, :], sel[:, h % HALF, :],
                              nmbd[e // HALF % 2][:, :, :].rearrange("p m t -> p (m t)"),
                              start=False, stop=True).then_inc(b_ready, 1)
                v = g - LAG_V
                if 0 <= v < B * H:
                    b, h = divmod(v, H)
                    r, i = divmod(h, PER)
                    rg = REG * b + r
                    if h == 0:
                        ended(pe, "proj", VW, b)
                    if i == 0:
                        since(pe, reg_ready, rg - 1)
                    pe.wait_ge(exp_ready, v + 1)
                    for m in range(M):
                        last = pe.matmul(PS[32 * m:32 * m + 32, 4 + rg % 2, 0:S], Vpad[b % 2][:, h, m, :],
                                         PT[v % PTN][:, m, :], start=(i == 0), stop=(h == region_last(r)),
                                         tile_position=(0, 32 * m))
                    last.then_inc(v_ready, 1)

            def down(n):
                half, j = divmod(n, FB)
                mj = min(P, F - j * P)
                pe.wait_ge(hL_ready, n + 1)
                if j == 0:
                    if half:
                        pe.wait_ge(y_added, 4)
                    else:
                        pe.wait_ge(exp_ready, B * H)
                        pe.wait_ge(max_ready, B * H)
                for t in range(4):
                    for k, (a, c) in enumerate(((hH, dH), (hH, dL), (hL, dH))):
                        last = pe.matmul(PS[:, t, :], a[n % 2][0:mj, t * S:t * S + S], c[j][0:mj, :],
                                         start=(j == 0 and k == 0), stop=(j == FB - 1 and k == 2))
                last.then_inc(y_ready, 1)

            pe.wait_ge(reg_ready, REG * B)
            for n in range(2 * FB):
                half, j = divmod(n, FB)
                mj = min(P, F - j * P)
                if n == 0:
                    ended(pe, *order[-2])
                    ended(pe, *order[-1])
                if j == 0:
                    pe.wait_ge(x2_in[half], 32)
                pe.wait_ge(ffw_low, 3 * (j + 1))
                since(pe, hf_ready, n - 1)
                for W, bank, s in (((gH, gL), 4, g_ready), ((uH, uL), 6, u_ready)):
                    product(PS[0:mj, bank + n % 2, :], lambda p, i: W[p][j][:, i * mj:i * mj + mj],
                            lambda p, i: x2[half][p][:, i, :], KB).then_inc(s, 1)
                if n >= 1:
                    down(n - 1)
            down(2 * FB - 1)


_OUTS = [((B, S, D), "float32")]


def kernel(**inputs):
    import numpy as _np
    import concourse.bacc as _bacc
    from concourse import mybir as _mybir
    from concourse.bass_utils import run_bass_kernel_spmd as _run

    a = {k: _np.asarray(v) for k, v in inputs.items()}
    rows = [h * M * DK + d * M + m
            for r in range(REG) for m in range(M) for h in range(PER * r, min(PER * r + PER, H)) for d in range(DK)]
    column = lambda v: v.reshape(KB, P).T
    laid = {
        "x": a["x"],
        "ctxT": a["ctx_4096"].transpose(0, 2, 1),
        "Wq": a["L0_xattn_Wq"], "Wk": a["L0_xattn_Wk"], "Wv": a["L0_xattn_Wv"],
        "WoT": a["L0_xattn_Wo"].T[rows],
        "bq": column(a["L0_xattn_bq"]), "bk": column(a["L0_xattn_bk"]), "bv": column(a["L0_xattn_bv"]),
        "bo": _np.broadcast_to(a["L0_xattn_bo"], (P, D)),
        "mix": _np.broadcast_to(a["L0_xattn_interference"][:, None], (H, DK, M, M)).reshape(H * DK * M, M),
        "amp": _np.broadcast_to(a["L0_xattn_amp"], (P, 1)),
        "WgT": a["L0_ffn_W_gate"].T, "WuT": a["L0_ffn_W_up"].T, "WdT": a["L0_ffn_W_down"].T,
    }
    nc = _bacc.Bacc("TRN2", target_bir_lowering=False, num_devices=1)
    arrays, args = {}, {}
    for name, v in laid.items():
        v = _np.ascontiguousarray(v)
        arrays[f"in_{name}_dram"] = v
        args[name] = nc.dram_tensor(f"in_{name}_dram", v.shape, _mybir.dt.from_np(v.dtype), kind="ExternalInput").ap()
    for i, (shape, dtype) in enumerate(_OUTS):
        args["out"] = nc.dram_tensor(f"out_{i}_dram", shape, _mybir.dt.from_np(_np.dtype(dtype)),
                                     kind="ExternalOutput").ap()
    build(nc, **args)
    r = _run(nc, [arrays], core_ids=[0])
    return r.results[0]["out_0_dram"]
```

```python
import concourse.bass as bass
from concourse import mybir
from contextlib import ExitStack

F32 = mybir.dt.float32
F32R = mybir.dt.float32r
ACT = mybir.ActivationFunctionType
ALU = mybir.AluOpType
AX = mybir.AxisListType

P = 128
B, S, D = 8, 128, 512
H, M, DK = 16, 4, 8
KB = D // P
GH = H // KB
F = 1376
FB = -(-F // P)
EPS = 1e-5
PARTS = 3
ROWS = M * PARTS * DK
PER = 3
REG = -(-H // PER)
LAG_B = 12
LAG_V = LAG_B + 2
HALF = H // 2
KST = 3
PTN = 3
TOK = 512
KW, QW, VW = range(3)
RC = 4
FIRST = -4
EARLY = 3
LEAD = 2


def region_last(r):
    return min(PER * r + PER, H) - 1


OPERANDS = dict(norm=-3, split_ctx=-1, proj_k=1, xT=1, stack_k=3, proj_q=5, stack_q=8, proj_v=15)
RESULTS = dict(shift_0=9, shift_1=18,
               norm_out_0=27, norm_out_1=31, oT=33, out=34, norm2=35, x2T=38)
PREPARE = dict(weights_v=-4, proj_v=-3, bias_v=-4, split_wo=-4, biasT=-4, bias_out=-1, batch_1=2)
WEIGHTS = dict(load=115, split=(120, 124, 129))
BLOCKS = dict(gate=(16, 20), up=(17, 22), split=25)


def plan():
    at = {}

    def place(step, *job):
        at.setdefault(max(step, FIRST), []).append(job)

    W = lambda w: [("W", w, k) for k in range(KB)]
    for job in (*W(KW), ("norm", 0), ("split_ctx", 0), ("bias", KW), ("proj", KW, 0), *W(QW), ("stack", KW, 0),
                ("xT", 0), ("bias", QW), ("proj", QW, 0), *W(VW)[:2], ("stack", QW, 0)):
        place(FIRST, *job)
    for job in W(VW)[2:]:
        place(PREPARE["weights_v"], *job)
    place(PREPARE["proj_v"], "proj", VW, 0)
    place(PREPARE["bias_v"], "bias", VW)
    place(PREPARE["split_wo"], "Wo")
    place(PREPARE["biasT"], "biasT")
    place(PREPARE["bias_out"], "bias_out")
    for b in range(B):
        t = H * (b - 1)
        late = PREPARE["batch_1"] if b == 1 else 0
        if b:
            place(t + OPERANDS["norm"], "norm", b)
            place(t + late + OPERANDS["split_ctx"], "split_ctx", b)
            place(t + late + OPERANDS["proj_k"], "proj", KW, b)
            place(t + late + OPERANDS["xT"], "xT", b)
            place(t + late + OPERANDS["stack_k"], "stack", KW, b)
            place(t + late + OPERANDS["proj_q"], "proj", QW, b)
            place(t + late + OPERANDS["stack_q"], "stack", QW, b)
            place(t + OPERANDS["proj_v"], "proj", VW, b)
        t += H
        place(t + RESULTS["shift_0"], "shift", b, 0)
        place(t + RESULTS["shift_1"], "shift", b, 1)
        place(t + RESULTS["norm_out_0"], "norm_out", b, 0)
        place(t + RESULTS["norm_out_1"], "norm_out", b, 1)
        place(t + RESULTS["oT"], "oT", b)
        place(t + RESULTS["out"], "out", b)
        place(t + RESULTS["norm2"], "norm2", b)
        place(t + RESULTS["x2T"], "x2T", b)
    for j in range(EARLY):
        place(WEIGHTS["load"], "ffw_load", j)
        place(WEIGHTS["split"][j], "ffw", j)
    t = H * B
    place(t + 1, "x2_load", 0)
    place(t + 1, "ffw_load", EARLY)
    for n in range(LEAD):
        place(t + BLOCKS["gate"][n], "gate", n)
        place(t + BLOCKS["up"][n], "up", n)
    place(t + BLOCKS["split"], "ffw", EARLY)
    return range(FIRST, max(at) + 1), at


def build(nc, x, ctxT, Wq, Wk, Wv, WoT, bq, bk, bv, bo, mix, amp, WgT, WuT, WdT, out):
    steps, at = plan()
    NO_BANK = ("split_ctx", "norm", "norm2", "Wo", "ffw", "ffw_load", "x2_load", "gate", "up")
    order = [j for g in steps for j in at.get(g, []) if j[0] not in NO_BANK]
    JOB = {j: n for n, j in enumerate(order)}
    first_jobs = sum(j in JOB for j in at[FIRST])
    BANK = [4 + n % 4 if n < first_jobs else 6 + n % 2 for n in range(len(order))]
    BEFORE = [max((i for i in range(n) if BANK[i] == BANK[n]), default=None) for n in range(len(order))]
    ON_ACT = ("W", "Wo", "xT", "stack", "oT", "x2T", "split_ctx", "shift", "biasT")
    every = [j for g in steps for j in at.get(g, [])]
    ACTED = {j: n + 1 for n, j in enumerate(j for j in every if j[0] in ON_ACT or j[:2] == ("proj", VW))}
    DONE = {j: n + 1 for n, j in enumerate(
        j for j in order if j[0] not in ("shift", "biasT", "norm_out") and j[:2] != ("proj", VW))}

    with ExitStack() as ctx:
        sem = lambda n: ctx.enter_context(nc.semaphore(n))
        scr = nc.dram_tensor("stack_scratch", [2, 2, M, PARTS, DK, H, S], F32, kind="Internal").ap()
        x2d = nc.dram_tensor("x2_scratch", [2, P, KB, B * S], F32, kind="Internal").ap()
        x1d = nc.dram_tensor("x1_scratch", [B, S, D], F32, kind="Internal").ap()
        PS = ctx.enter_context(nc.psum_tensor("PS", [P, 8, 512], F32))

        def alloc(stack):
            return lambda n, s, d=F32: stack.enter_context(nc.sbuf_tensor(n, s, d))

        sb = alloc(ctx)
        ident = sb("ident", [P, P])
        neghalf = sb("neghalf", [P, 1])

        one = ExitStack()
        sb = alloc(one)
        WH, WL = [None] * 4, [None] * 4
        for w in range(3):
            WH[w], WL[w] = sb(f"WH{w}", [P, KB, D], F32R), sb(f"WL{w}", [P, KB, D], F32R)
        Kbd = [sb(f"Kbd{i}", [ROWS, GH, M, S], F32R) for i in range(2)]
        Kst = [sb("Kst0", [ROWS, H, S], F32R)]
        Qst = [sb("Qst0", [ROWS, H, S], F32R)]
        prep = ExitStack()
        sbp = alloc(prep)
        Wn = [None] * 4
        for w in (2, 3, 0, 1):
            Wn[w] = sbp(f"Wn{w}", [P, KB, D])
        BD = sbp("BD", [P, KB, P])
        bwide = sbp("bwide", [P, 3, KB, P])
        prep.close()
        Qbd = [sb(f"Qbd{i}", [ROWS, GH, M, S], F32R) for i in range(2)]
        Kst += [sb(f"Kst{i}", [ROWS, H, S], F32R) for i in range(1, KST)]
        Qst += [sb("Qst1", [ROWS, H, S], F32R)]
        WH[3], WL[3] = sb("WH3", [P, KB, D], F32R), sb("WL3", [P, KB, D], F32R)
        mixs = sb("mixs", [P, KB, M])
        amps = sb("amps", [P, 1])
        bcol = sb("bcol", [P, 3, KB])
        blk = sb("blk", [P, P // M])
        selc = sb("selc", [64, HALF])
        bias = [sb(f"bias{w}", [P, D]) for w in range(2)]
        bob = sb("bob", [P, D])
        mask96 = sb("mask96", [ROWS, M])
        mask64 = sb("mask64", [64, M])
        sel = sb("sel", [64, HALF, P], F32R)
        Vpad = [sb(f"Vpad{i}", [P, H, M, 32]) for i in range(2)]
        xin = sb("xin", [P, D])
        xres = sb("xres", [P, D])
        cin = sb("cin", [P, KB, S])
        cH = sb("cH", [P, KB, S], F32R)
        cL = sb("cL", [P, KB, S], F32R)
        stats = sb("stats", [P, 6])
        mv = sb("mv", [P, 2])
        ve = sb("ve", [P, 1])
        rstd = sb("rstd", [P, 1])
        xTH = sb("xTH", [P, KB, S], F32R)
        xTL = sb("xTL", [P, KB, S], F32R)
        kq = sb("kq", [P, D])
        kqH = [sb(f"kqH{w}", [P, M, S], F32R) for w in range(2)]
        kqL = [sb(f"kqL{w}", [P, M, S], F32R) for w in range(2)]
        mx = sb("mx", [P, M, H])
        nm = sb("nm", [P, M, 2, HALF], F32R)
        nmbd = [sb(f"nmbd{i}", [64, M, S], F32R) for i in range(2)]
        prep = ExitStack()
        sbp = alloc(prep)
        bvo = sbp("bvo", [P, D])
        bvT = sbp("bvT", [P, KB, P])
        prep.close()
        PT = [sb(f"PT{i}", [P, M, S]) for i in range(PTN)]
        reg = [sb(f"reg{i}", [P, S]) for i in range(REG)]
        rec = sb("rec", [P, RC * M, PER])
        on = sb("on", [P, D])
        oTH = sb("oTH", [P, KB, S], F32R)
        oTL = sb("oTL", [P, KB, S], F32R)
        stats2 = sb("stats2", [P, 6])
        mv2 = sb("mv2", [P, 2])
        ve2 = sb("ve2", [P, 1])
        rstd2 = sb("rstd2", [P, 1])
        one.close()

        two = ExitStack()
        sb = alloc(two)
        fin = [[sb(f"fin{i}{k}", [P, D]) for k in range(3)] for i in range(2)]
        gH, gL, uH, uL, dH, dL = fw = [[] for _ in range(6)]

        def block_of_weights(j):
            for k, name in enumerate(("gH", "gL", "uH", "uL", "dH", "dL")):
                fw[k].append(sb(f"{name}{j}", [P, D], F32R))

        for j in range(EARLY):
            block_of_weights(j)
        x2 = [[sb(f"x2{p}{i}", [P, KB, TOK], F32R) for p in "HL"] for i in range(2)]
        th = sb("th", [P, TOK])
        hu = sb("hu", [P, TOK])
        hf = sb("hf", [P, TOK])
        hH = [sb(f"hH{i}", [P, TOK], F32R) for i in range(2)]
        hL = [sb(f"hL{i}", [P, TOK], F32R) for i in range(2)]
        for j in range(EARLY, FB):
            block_of_weights(j)
        x1in = [sb(f"x1in{i}", [P, D]) for i in range(4)]
        yo = [sb(f"yo{i}", [P, D]) for i in range(4)]
        two.close()

        mix_in, bias_in, bo_in = [sem(n) for n in ("mix_in", "bias_in", "bo_in")]
        wk_in = [sem(f"wk_in{k}") for k in range(KB)]
        w_in = [None] + [sem(f"w_in{w}") for w in range(1, 4)]
        x_in, c_in, xres_in = sem("x_in"), sem("c_in"), sem("xres_in")
        stack_written = [sem(f"stack_written{w}") for w in range(2)]
        stack_in = [[sem(f"stack_in{w}{i}") for i in range((KST, 2)[w])] for w in range(2)]
        x1_written = sem("x1_written")
        pool_setup, dve_setup, mixed, wide, wo_low = [
            sem(n) for n in ("pool_setup", "dve_setup", "mixed", "wide", "wo_low")]
        job_ready, dve_done, act_done = sem("job_ready"), sem("dve_done"), sem("act_done")
        low_ctx, stat, rstd_ready, xn_ready = sem("low_ctx"), sem("stat"), sem("rstd_ready"), sem("xn_ready")
        nm_ready, rec_ready, on_ready, resid = sem("nm_ready"), sem("rec_ready"), sem("on_ready"), sem("resid")
        a_ready, max_ready, b_ready, exp_ready, v_ready, reg_ready = [
            sem(n) for n in ("a_ready", "max_ready", "b_ready", "exp_ready", "v_ready", "reg_ready")]
        bd_built = [sem("kbd_built"), sem("qbd_built")]
        x1_in = [sem(f"x1_in{i}") for i in range(4)]
        stat2, rstd2_ready, x2n_ready = [sem(n) for n in ("stat2", "rstd2_ready", "x2n_ready")]
        x2_written, x2_in = sem("x2_written"), [sem(f"x2_in{i}") for i in range(2)]
        ffw_in = [sem(f"ffw_in{i}") for i in range(2)]
        ffw_high, ffw_low = sem("ffw_high"), sem("ffw_low")
        g_ready, u_ready, th_ready, hu_ready, hf_ready, hH_ready, hL_ready, y_ready = [
            sem(n) for n in ("g_ready", "u_ready", "th_ready", "hu_ready", "hf_ready", "hH_ready", "hL_ready", "y_ready")]
        y_added = sem("y_added")
        out_written = [sem(f"out_written{i}") for i in range(4)]

        def since(eng, s, n):
            if n > 0:
                eng.wait_ge(s, n)

        def ended(eng, *j):
            if j[0] == "norm_out":
                eng.wait_ge(on_ready, 3 * j[1] + 1 + 2 * j[2])
            elif j in DONE:
                eng.wait_ge(dve_done, DONE[j])
            else:
                eng.wait_ge(act_done, ACTED[j])

        def multiplied(eng, *j):
            eng.wait_ge(job_ready, JOB[j] + 1)

        def downs(n):
            return n + 1 + 3 * ((n + 1) // FB)

        block = ctx.enter_context(nc.Block())

        @block.sync
        def _(sp):
            sp.dma_start(mixs[:, :, :], mix.rearrange("(g p) j -> p g j", p=P)).then_inc(mix_in, 16)
            sp.dma_start(amps[:, :], amp).then_inc(mix_in, 16)
            columns = lambda v: v.rearrange("(k p) c -> p k c", p=P)
            for k in range(KB):
                sp.dma_start(Wn[KW][:, :, k * P:k * P + P], columns(Wk)[:, :, k * P:k * P + P]
                             ).then_inc(wk_in[k], 16)
            sp.dma_start(xin[:, :], x[0]).then_inc(x_in, 16)
            sp.dma_start(cin[:, :, :], columns(ctxT[0])).then_inc(c_in, 16)
            for w, bb in enumerate((bk, bq, bv)):
                sp.dma_start(bcol[:, w, :], bb).then_inc(bias_in, 16)
            sp.dma_start(Wn[QW][:, :, :], columns(Wq)).then_inc(w_in[QW], 16)
            sp.dma_start(Wn[VW][:, :, :], columns(Wv)).then_inc(w_in[VW], 16)
            sp.dma_start(Wn[3][:, :, :], columns(WoT)).then_inc(w_in[3], 16)
            sp.dma_start(bob[:, :], bo).then_inc(bo_in, 16)

            def load_weights(j):
                mj = min(P, F - j * P)
                since(sp, ffw_low, 3 * (j - 1))
                for t, W in enumerate((WgT, WuT)):
                    sp.dma_start(fin[j % 2][t][:, 0:KB * mj].rearrange("p (k f) -> p k f", k=KB),
                                 W[:, j * P:j * P + mj].rearrange("(k p) f -> p k f", p=P)).then_inc(ffw_in[j % 2], 16)
                sp.dma_start(fin[j % 2][2][0:mj, :], WdT[j * P:j * P + mj, :]).then_inc(ffw_in[j % 2], 16)

            def load_x2(half):
                for p in range(2):
                    sp.dma_start(x2[half][p][:, :, :].bitcast(F32), x2d[p, :, :, half * TOK:half * TOK + TOK]
                                 ).then_inc(x2_in[half], 16)

            for g in steps:
                for j in at.get(g, []):
                    b = j[-1]
                    if j[0] == "split_ctx" and b:
                        sp.wait_ge(low_ctx, b)
                        sp.dma_start(cin[:, :, :], ctxT[b].rearrange("(k p) t -> p k t", p=P)).then_inc(c_in, 16)
                    if j[0] == "xT" and b + 1 < B:
                        multiplied(sp, *j)
                        sp.dma_start(xin[:, :], x[b + 1]).then_inc(x_in, 16)
                    if j[0] == "stack":
                        w = j[1]
                        ended(sp, *j)
                        own = scr[w, b % 2]
                        for part, src in enumerate(((kqH, kqL, kqH), (kqH, kqH, kqL))[w]):
                            sp.dma_start(own[:, part].rearrange("m d h t -> (d h) m t"),
                                         src[w][:, :, :].bitcast(F32)).then_inc(stack_written[w], 16)
                        sp.wait_ge(stack_written[w], 16 * PARTS * (b + 1))
                        ring = (KST, 2)[w]
                        if b == 1:
                            ended(sp, "bias_out")
                            sp.wait_ge(wo_low, 1)
                        if b >= ring:
                            sp.wait_ge((b_ready, a_ready)[w], H * (b - ring + 1))
                            sp.wait_ge(bd_built[w], M * KB * (b - ring + 1))
                        sp.dma_start((Kst, Qst)[w][b % ring][:, :, :].rearrange("p h t -> p (h t)").bitcast(F32),
                                     own.rearrange("m s d h t -> (m s d) (h t)")).then_inc(stack_in[w][b % ring], 16)
                    if j[0] == "oT":
                        since(sp, x2n_ready, b)
                        since(sp, x1_written, 16 * b)
                        sp.dma_start(xres[:, :], x[b]).then_inc(xres_in, 16)
                    if j[0] == "out":
                        ended(sp, *j)
                        sp.dma_start(x1d[b], xres[:, :]).then_inc(x1_written, 16)
                    if j[0] == "x2T":
                        ended(sp, *j)
                        for p, src in enumerate((oTH, oTL)):
                            sp.dma_start(x2d[p, :, :, b * S:b * S + S], src[:, :, :].bitcast(F32)
                                         ).then_inc(x2_written, 16)
                    if j[0] == "ffw_load":
                        if b == 0:
                            ended(sp, "proj", VW, B - 1)
                        load_weights(b)
                    if j[0] == "x2_load":
                        sp.wait_ge(a_ready, B * H)
                        sp.wait_ge(x2_written, 32 * 4)
                        load_x2(0)
            load_weights(EARLY + 1)
            sp.wait_ge(x2_written, 32 * B)
            sp.wait_ge(b_ready, B * H)
            load_x2(1)
            for j in range(EARLY + 2, FB):
                load_weights(j)
            sp.wait_ge(x1_written, 16 * B)
            for b in range(4):
                sp.dma_start(x1in[b][:, :], x1d[b]).then_inc(x1_in[b], 16)
            for b in range(4):
                sp.wait_ge(y_added, b + 1)
                sp.dma_start(out[b], yo[b][:, :]).then_inc(out_written[b], 16)
                sp.dma_start(x1in[b][:, :], x1d[b + 4]).then_inc(x1_in[b], 16)
            for b in range(4, B):
                sp.wait_ge(y_added, b + 1)
                sp.dma_start(out[b], yo[b - 4][:, :]).then_inc(out_written[b - 4], 16)
            for written in out_written:
                sp.wait_ge(written, 32)

        @block.gpsimd
        def _(pool):
            pool.memset(ident[:, :], 0.0).then_inc(pool_setup, 1)
            pool.memset(neghalf[:, :], -0.5).then_inc(pool_setup, 1)
            pool.wait_ge(pool_setup, 2)
            pool.affine_select(out=ident[:, :], in_=ident[:, :], compare_op=ALU.not_equal, fill=1.0, base=0,
                               pattern=[[-1, P]], channel_multiplier=1).then_inc(pool_setup, 1)
            for v in Vpad:
                pool.memset(v[:, :, :, :], 0.0).then_inc(pool_setup, 1)
            pool.wait_ge(pool_setup, 5)
            for v in Vpad:
                for i in range(PER):
                    pool.memset(v[:, i:H:PER, :, DK * PER + i], 1.0).then_inc(pool_setup, 1)

            def spread(w, q):
                b, u = q // KB, q % KB
                ring = (KST, 2)[w]
                pool.wait_ge(stack_in[w][b % ring], 16 * (b // ring + 1))
                since(pool, (a_ready, b_ready)[w], GH * (q - 1))
                st, bd = ((Kst, Kbd), (Qst, Qbd))[w]
                if (w, q) == (QW, 0):
                    ended(pool, "bias_out")
                    pool.wait_ge(wo_low, 1)
                if (w, q) == (KW, 0):
                    pool.wait_ge(dve_setup, 2)
                for m in range(M):
                    pool.tensor_scalar(bd[q % 2][:, :, m, :], st[b % ring][:, GH * u:GH * u + GH, :].bitcast(F32),
                                       mask96[:, m:m + 1], 1.0, ALU.mult, ALU.mult).then_inc(bd_built[w], 1)

            def power(b):
                pool.wait_ge(stat, 3 * b + 3)
                pool.tensor_tensor(rstd[:, :], ve[:, :], neghalf[:, :], ALU.pow).then_inc(rstd_ready, 1)

            def power2(b):
                pool.wait_ge(stat2, 3 * b + 3)
                pool.tensor_tensor(rstd2[:, :], ve2[:, :], neghalf[:, :], ALU.pow).then_inc(rstd2_ready, 1)

            power(0)
            spread(KW, 0)
            for q in range(KB * (B + 2) + 2):
                b, u = divmod(q, KB)
                if u == 0 and 0 < b + 1 < B:
                    power(b + 1)
                if u == 1 and 0 <= b - 2 < B:
                    power2(b - 2)
                if 0 <= q - 2 < KB * B:
                    spread(QW, q - 2)
                if q + 1 < KB * B:
                    spread(KW, q + 1)

        @block.scalar
        def _(act):
            def high(dst, src):
                act.activation(dst, src, ACT.Copy).then_inc(act_done, 1)

            def split_h_high(n):
                mj = min(P, F - (n % FB) * P)
                act.wait_ge(hf_ready, n + 1)
                if n >= 2:
                    act.wait_ge(y_ready, downs(n - 2))
                act.activation(hH[n % 2][0:mj, :], hf[0:mj, :], ACT.Copy).then_inc(hH_ready, 1)

            def split_weights_high(j):
                mj = min(P, F - j * P)
                act.wait_ge(ffw_in[j % 2], 48 * (j // 2 + 1))
                for t, W in enumerate((gH, uH)):
                    act.activation(W[j][:, 0:KB * mj], fin[j % 2][t][:, 0:KB * mj], ACT.Copy).then_inc(ffw_high, 1)
                act.activation(dH[j][0:mj, :], fin[j % 2][2][0:mj, :], ACT.Copy).then_inc(ffw_high, 1)

            def half_tanh(n):
                mj = min(P, F - (n % FB) * P)
                act.wait_ge(g_ready, n + 1)
                since(act, hu_ready, n)
                act.activation(th[0:mj, :], PS[0:mj, n % 2, :], ACT.Tanh, scale=0.5).then_inc(th_ready, 1)

            act.wait_ge(bias_in, 48)
            act.activation(bwide[:, :, :, :].rearrange("p w g t -> p (w g) t"),
                           bcol[:, :, :].rearrange("p w g -> p (w g)").unsqueeze(2).broadcast_to([P, 3 * KB, P]),
                           ACT.Copy).then_inc(wide, 1)
            for g in steps:
                for j in at.get(g, []):
                    b = j[-1]
                    n = JOB.get(j)
                    ps = None if n is None else PS[:, BANK[n], :]
                    if j[0] == "up":
                        half_tanh(j[1])
                        split_h_high(j[1])
                    if j[0] == "W":
                        _, w, k = j
                        multiplied(act, *j)
                        high(WH[w][:, k, :].rearrange("p (m d h) -> p m d h", m=M, d=DK),
                             ps.rearrange("p (h d m) -> p m d h", h=H, d=DK))
                    if j[0] == "Wo":
                        act.wait_ge(w_in[3], 16)
                        high(WH[3][:, :, :], Wn[3][:, :, :])
                    if j[0] == "biasT":
                        multiplied(act, *j)
                        high(bvT[:, :, :], ps.rearrange("p (k t) -> p k t", k=KB))
                    if j[0] == "split_ctx":
                        act.wait_ge(c_in, 16 * (b + 1))
                        if b:
                            multiplied(act, "proj", VW, b - 1)
                        high(cH[:, :, :], cin[:, :, :])
                    if j[0] == "xT":
                        multiplied(act, *j)
                        high(xTH[:, :, :], ps.rearrange("p (k t) -> p k t", k=KB))
                    if j[0] == "stack":
                        w = j[1]
                        multiplied(act, *j)
                        since(act, stack_written[w], 16 * PARTS * b)
                        high(kqH[w][:, :, :], ps.rearrange("p (m t) -> p m t", m=M))
                    if j[:2] == ("proj", VW):
                        multiplied(act, *j)
                        act.wait_ge(pool_setup, 11)
                        since(act, v_ready, H * (b - 1))
                        for i in range(PER):
                            last = act.activation(Vpad[b % 2][:, i:H:PER, :, DK * i:DK * i + DK],
                                                  ps.rearrange("p (m d h) -> p h m d", m=M, d=DK)[:, i:H:PER],
                                                  ACT.Copy)
                        last.then_inc(act_done, 1)
                    if j[0] == "shift":
                        _, b, half = j
                        k = 2 * b + half
                        multiplied(act, *j)
                        since(act, b_ready, HALF * (k - 1))
                        for m in range(M):
                            last = act.activation(nmbd[k % 2][:, m, :], ps[0:64, 0:S], ACT.Copy,
                                                  scale=mask64[:, m:m + 1])
                        last.then_inc(act_done, 1)
                    if j[0] == "oT":
                        multiplied(act, *j)
                        since(act, x2_written, 32 * b)
                        high(oTH[:, :, :], ps.rearrange("p (k t) -> p k t", k=KB))
                    if j[0] == "x2T":
                        multiplied(act, *j)
                        high(oTH[:, :, :], ps.rearrange("p (k t) -> p k t", k=KB))
                    if j[0] == "ffw":
                        if b == 0:
                            ended(act, "proj", VW, B - 1)
                        if b == EARLY:
                            act.wait_ge(b_ready, B * H)
                        split_weights_high(b)
                e = g - LAG_B
                if 0 <= e < B * H:
                    act.wait_ge(b_ready, e + 1)
                    since(act, v_ready, e - PTN + 1)
                    act.activation(PT[e % PTN][:, :, :], PS[:, 2 + e % 2, :].rearrange("p (m t) -> p m t", m=M),
                                   ACT.Exp, scale=DK ** -0.5).then_inc(exp_ready, 1)
                b, h = divmod(g - LAG_V - 1, H)
                if 0 <= b < B and h in [region_last(r) for r in range(REG)]:
                    r = h // PER
                    act.wait_ge(v_ready, H * b + h + 1)
                    if b:
                        multiplied(act, "norm_out", b - 1, int(r >= RC))
                    act.activation(reg[r][:, :], PS[:, 4 + (REG * b + r) % 2, 0:S], ACT.Copy).then_inc(reg_ready, 1)
            for n in range(LEAD, 2 * FB):
                if n == LEAD:
                    ended(act, "x2T", B - 1)
                half_tanh(n)
                split_h_high(n)
                if EARLY < n + 2 < FB:
                    split_weights_high(n + 2)

        @block.vector
        def _(dve):
            dve.wait_ge(pool_setup, 3)
            dve.tensor_reduce(blk[:, :], ident[:, :].rearrange("p (k j) -> p k j", j=M),
                              AX.X, ALU.add).then_inc(dve_setup, 1)
            dve.tensor_reduce(mask96[:, :], ident[0:ROWS, 0:ROWS].rearrange("p (m j) -> p m j", m=M),
                              AX.X, ALU.add).then_inc(dve_setup, 1)
            dve.wait_ge(mix_in, 32)
            dve.tensor_scalar(mixs[:, :, :], mixs[:, :, :], amps[:, 0:1], 0.1, ALU.mult, ALU.mult).then_inc(mixed, 1)
            dve.wait_ge(mixed, 1)
            dve.wait_ge(dve_setup, 1)
            for g in range(KB):
                dve.tensor_tensor(BD[:, g, :].rearrange("p (k j) -> p k j", j=M),
                                  mixs[:, g, :].unsqueeze(1).broadcast_to([P, P // M, M]),
                                  blk[:, :].unsqueeze(2).broadcast_to([P, P // M, M]), ALU.mult).then_inc(mixed, 1)
            dve.wait_ge(mixed, 1 + KB)
            for g in range(KB):
                dve.tensor_tensor(BD[:, g, :], BD[:, g, :], ident[:, :], ALU.add).then_inc(mixed, 1)

            def shift_masks():
                dve.tensor_reduce(mask64[:, :], ident[0:64, 0:64].rearrange("p (m j) -> p m j", m=M),
                                  AX.X, ALU.add).then_inc(dve_setup, 1)
                dve.tensor_reduce(selc[:, :], ident[0:64, 0:64].rearrange("p (j h) -> p h j", h=HALF),
                                  AX.X, ALU.add).then_inc(dve_setup, 1)
                dve.wait_ge(dve_setup, 4)
                dve.tensor_copy(sel[:, :, :], selc[:, :].unsqueeze(2).broadcast_to([64, HALF, P])
                                ).then_inc(dve_setup, 1)

            def low(j, dst, src, hi):
                dve.wait_ge(act_done, ACTED[j])
                return dve.tensor_tensor(dst, src, hi.bitcast(F32), ALU.subtract)

            def split_weights_low(j):
                mj = min(P, F - j * P)
                for t, (lo, hi, rows, cols) in enumerate(
                        ((gL, gH, P, KB * mj), (uL, uH, P, KB * mj), (dL, dH, mj, D))):
                    dve.wait_ge(ffw_high, 3 * j + t + 1)
                    dve.tensor_tensor(lo[j][0:rows, 0:cols], fin[j % 2][t][0:rows, 0:cols],
                                      hi[j][0:rows, 0:cols].bitcast(F32), ALU.subtract).then_inc(ffw_low, 1)

            def moments(rows, arrived, count, st, m, v, done, b):
                dve.wait_ge(arrived, count)
                dve.bn_stats(st[:, :], rows[:, :]).then_inc(done, 1)
                dve.wait_ge(done, 3 * b + 1)
                dve.bn_aggr(m[:, :], st[:, :]).then_inc(done, 1)
                dve.wait_ge(done, 3 * b + 2)
                dve.tensor_scalar(v[:, :], m[:, 1:2], EPS, None, ALU.add).then_inc(done, 1)

            def gated(n):
                mj = min(P, F - (n % FB) * P)
                dve.wait_ge(th_ready, n + 1)
                since(dve, hf_ready, n)
                dve.scalar_tensor_tensor(out=hu[0:mj, :], in0=th[0:mj, :], scalar=1.0, in1=PS[0:mj, n % 2, :],
                                         op0=ALU.add, op1=ALU.mult).then_inc(hu_ready, 1)
                dve.wait_ge(hu_ready, n + 1)
                dve.wait_ge(u_ready, n + 1)
                since(dve, hL_ready, n)
                dve.scalar_tensor_tensor(out=hf[0:mj, :], in0=hu[0:mj, :], scalar=0.5, in1=PS[0:mj, 2 + n % 2, :],
                                         op0=ALU.mult, op1=ALU.mult).then_inc(hf_ready, 1)
                dve.wait_ge(hH_ready, n + 1)
                dve.tensor_tensor(hL[n % 2][0:mj, :], hf[0:mj, :], hH[n % 2][0:mj, :].bitcast(F32), ALU.subtract
                                  ).then_inc(hL_ready, 1)

            rec_used = [0]
            for g in steps:
                if 0 <= g < B * H:
                    b, h = divmod(g, H)
                    dve.wait_ge(a_ready, g + 1)
                    dve.tensor_reduce(mx[:, :, h], PS[:, g % 2, :].rearrange("p (m t) -> p m t", m=M),
                                      AX.X, ALU.max, negate=True).then_inc(max_ready, 1)
                for j in at.get(g, []):
                    b = j[-1]
                    n = JOB.get(j)
                    ps = None if n is None else PS[:, BANK[n], :]
                    if j[0] == "up":
                        gated(j[1])
                    if j[0] == "W":
                        _, w, k = j
                        low(j, WL[w][:, k, :].rearrange("p (m d h) -> p m d h", m=M, d=DK),
                            ps.rearrange("p (h d m) -> p m d h", h=H, d=DK),
                            WH[w][:, k, :].rearrange("p (m d h) -> p m d h", m=M, d=DK)).then_inc(dve_done, 1)
                    if j[0] == "bias" and j[1] != VW:
                        multiplied(dve, *j)
                        dve.tensor_copy(bias[j[1]][:, :].rearrange("p (m d h) -> p m d h", m=M, d=DK),
                                        ps.rearrange("p (h d m) -> p m d h", h=H, d=DK)).then_inc(dve_done, 1)
                    if j == ("bias", VW):
                        multiplied(dve, *j)
                        for r in range(REG):
                            k = min(PER, H - PER * r)
                            c0 = r * PER * M * DK
                            last = dve.tensor_copy(
                                bvo[:, c0:c0 + k * M * DK].rearrange("p (m i d) -> p m i d", m=M, i=k),
                                ps[:, c0:c0 + k * M * DK].rearrange("p (i d m) -> p m i d", m=M, i=k))
                        last.then_inc(dve_done, 1)
                    if j[0] == "bias_out":
                        multiplied(dve, *j)
                        dve.wait_ge(bo_in, 16)
                        dve.tensor_tensor(bob[:, :], ps, bob[:, :], ALU.add).then_inc(dve_done, 1)
                    if j[0] == "Wo":
                        low(j, WL[3][:, :, :], Wn[3][:, :, :], WH[3][:, :, :]).then_inc(wo_low, 1)
                        shift_masks()
                    if j[0] == "split_ctx":
                        low(j, cL[:, :, :], cin[:, :, :], cH[:, :, :]).then_inc(low_ctx, 1)
                    if j[0] == "norm":
                        moments(xin, x_in, 16 * (b + 1), stats, mv, ve, stat, b)
                    if j[:2] == ("proj", KW):
                        dve.wait_ge(rstd_ready, b + 1)
                        dve.tensor_scalar(xin[:, :], xin[:, :], mv[:, 0:1], rstd[:, 0:1],
                                          ALU.subtract, ALU.mult).then_inc(xn_ready, 1)
                    if j[0] == "proj" and j[1] != VW:
                        multiplied(dve, *j)
                        if b == 0:
                            ended(dve, "bias", j[1])
                        dve.tensor_tensor(kq[:, :], ps, bias[j[1]][:, :], ALU.add).then_inc(dve_done, 1)
                    if j[0] == "xT":
                        low(j, xTL[:, :, :], ps.rearrange("p (k t) -> p k t", k=KB), xTH[:, :, :]
                            ).then_inc(dve_done, 1)
                    if j[0] == "stack":
                        w = j[1]
                        low(j, kqL[w][:, :, :], ps.rearrange("p (m t) -> p m t", m=M), kqH[w][:, :, :]
                            ).then_inc(dve_done, 1)
                    if j[0] == "norm_out":
                        _, b, c = j
                        multiplied(dve, *j)
                        for r0, nr, k in (((0, RC, PER),), ((RC, REG - RC - 1, PER), (REG - 1, 1, H - PER * (REG - 1)))
                                          )[c]:
                            cols = ps[:, (r0 - RC * c) * P:(r0 - RC * c + nr) * P].rearrange("p (s c) -> p s c", c=32)
                            if rec_used[0]:
                                dve.wait_ge(on_ready, rec_used[0])
                            rec_used[0] += 1
                            sums = rec[:, 0:nr * M, 0:k]
                            dve.reciprocal(sums, cols[:, :, DK * PER:DK * PER + k]).then_inc(rec_ready, 1)
                            dve.wait_ge(rec_ready, rec_used[0])
                            c0 = r0 * PER * M * DK
                            dve.tensor_tensor(
                                on[:, c0:c0 + nr * k * M * DK].rearrange("p (s i d) -> p s i d", s=nr * M, i=k),
                                cols[:, :, 0:DK * k].rearrange("p s (i d) -> p s i d", i=k),
                                sums.unsqueeze(3).broadcast_to([P, nr * M, k, DK]), ALU.mult).then_inc(on_ready, 1)
                    if j[0] == "oT":
                        low(j, oTL[:, :, :], ps.rearrange("p (k t) -> p k t", k=KB), oTH[:, :, :]
                            ).then_inc(dve_done, 1)
                    if j[0] == "out":
                        dve.wait_ge(xres_in, 16 * (b + 1))
                        dve.tensor_tensor(xres[:, :], xres[:, :], bob[:, :], ALU.add).then_inc(resid, 1)
                        dve.wait_ge(resid, b + 1)
                        multiplied(dve, *j)
                        dve.tensor_tensor(xres[:, :], ps, xres[:, :], ALU.add).then_inc(dve_done, 1)
                        moments(xres, dve_done, DONE[j], stats2, mv2, ve2, stat2, b)
                    if j[0] == "norm2":
                        dve.wait_ge(rstd2_ready, b + 1)
                        if b:
                            multiplied(dve, "x2T", b - 1)
                        dve.tensor_scalar(on[:, :], xres[:, :], mv2[:, 0:1], rstd2[:, 0:1],
                                          ALU.subtract, ALU.mult).then_inc(x2n_ready, 1)
                    if j[0] == "x2T":
                        low(j, oTL[:, :, :], ps.rearrange("p (k t) -> p k t", k=KB), oTH[:, :, :]
                            ).then_inc(dve_done, 1)
                    if j[0] == "ffw":
                        split_weights_low(b)
                b, h = divmod(g, H)
                if 0 <= b < B and h in (HALF - 1, H - 1):
                    k = 2 * b + h // HALF
                    mine = mx[:, :, h + 1 - HALF:h + 1]
                    dve.wait_ge(max_ready, g + 1)
                    if k:
                        multiplied(dve, "shift", (k - 1) // 2, (k - 1) % 2)
                    dve.tensor_copy(nm[:, :, 0, :], mine).then_inc(nm_ready, 1)
                    dve.wait_ge(nm_ready, 2 * k + 1)
                    dve.tensor_tensor(nm[:, :, 1, :], mine, nm[:, :, 0, :].bitcast(F32), ALU.subtract
                                      ).then_inc(nm_ready, 1)
            for n in range(LEAD, 2 * FB):
                gated(n)
                if EARLY < n + 2 < FB:
                    split_weights_low(n + 2)
                if n in (FB, 2 * FB - 1):
                    half = int(n > FB)
                    for t in range(4):
                        dve.wait_ge(y_ready, downs(FB * (half + 1) - 2) + t + 1)
                        dve.wait_ge(x1_in[t], 16 * (half + 1))
                        if half:
                            dve.wait_ge(out_written[t], 16)
                        dve.tensor_tensor(yo[t][:, :], PS[:, 4 + t, :], x1in[t][:, :], ALU.add).then_inc(y_added, 1)

        @block.tensor
        def _(pe):
            def product(out_, lhs, rhs, n):
                k = 0
                for i in range(n):
                    for l, r in ((0, 0), (0, 1), (1, 0)):
                        last = pe.matmul(out_, lhs(l, i), rhs(r, i), start=(k == 0), stop=(k == 3 * n - 1))
                        k += 1
                return last

            def gate_or_up(n, up):
                half, j = divmod(n, FB)
                mj = min(P, F - j * P)
                if n >= 2:
                    pe.wait_ge((hu_ready, hf_ready)[up], n - 1)
                elif up:
                    pe.wait_ge(exp_ready, B * H)
                else:
                    pe.wait_ge(max_ready, B * H)
                if not up:
                    if j == 0:
                        pe.wait_ge(x2_in[half], 32)
                    pe.wait_ge(ffw_low, 3 * (j + 1))
                W = ((gH, gL), (uH, uL))[up]
                product(PS[0:mj, 2 * up + n % 2, :], lambda p, i: W[p][j][:, i * mj:i * mj + mj],
                        lambda p, i: x2[half][p][:, i, :], KB).then_inc((g_ready, u_ready)[up], 1)

            for g in steps:
                if 0 <= g < B * H:
                    b, h = divmod(g, H)
                    if h == 0:
                        pe.wait_ge(stack_in[QW][b % 2], 16 * (b // 2 + 1))
                    if h % GH == 0:
                        pe.wait_ge(bd_built[KW], M * (g // GH + 1))
                    since(pe, max_ready, g - 1)
                    pe.matmul(PS[:, g % 2, :], Qst[b % 2][:, h, :],
                              Kbd[g // GH % 2][:, h % GH].rearrange("p m t -> p (m t)"),
                              start=True, stop=True).then_inc(a_ready, 1)
                for j in at.get(g, []):
                    b = j[-1]
                    if j[0] in ("gate", "up"):
                        gate_or_up(j[1], int(j[0] == "up"))
                    n = JOB.get(j)
                    if n is None:
                        continue
                    ps = PS[:, BANK[n], :]
                    if BEFORE[n] is not None:
                        ended(pe, *order[BEFORE[n]])
                    if j[0] == "W":
                        _, w, k = j
                        pe.wait_ge(wk_in[k] if w == KW else w_in[w], 16)
                        pe.wait_ge(mixed, 1 + 2 * KB)
                        for f in range(KB):
                            last = pe.matmul(ps[:, f * P:f * P + P], Wn[w][:, f, k * P:k * P + P], BD[:, f, :],
                                             start=True, stop=True)
                    if j[0] == "bias":
                        pe.wait_ge(wide, 1)
                        for f in range(KB):
                            last = pe.matmul(ps[:, f * P:f * P + P], bwide[:, j[1], f, :], BD[:, f, :],
                                             start=True, stop=True)
                    if j[0] == "biasT":
                        ended(pe, "bias", VW)
                        for k in range(KB):
                            last = pe.transpose(ps[:, k * S:k * S + S], bvo[:, k * P:k * P + P], ident[:, :])
                    if j[0] == "bias_out":
                        ended(pe, "biasT")
                        pe.wait_ge(w_in[3], 16)
                        for k in range(KB):
                            last = pe.matmul(ps, bvT[:, k, :], Wn[3][:, k, :], start=(k == 0), stop=(k == KB - 1))
                    if j[0] == "proj":
                        w = j[1]
                        if b == 0:
                            ended(pe, "W", w, KB - 1)
                        if w == QW:
                            ended(pe, "xT", b)
                            X = (xTH, xTL)
                        else:
                            pe.wait_ge(low_ctx, b + 1)
                            X = (cH, cL)
                        last = product(ps, lambda p, i: X[p][:, i, :], lambda p, i: (WH, WL)[p][w][:, i, :], KB)
                    if j[0] == "xT":
                        pe.wait_ge(xn_ready, b + 1)
                        for k in range(KB):
                            last = pe.transpose(ps[:, k * S:k * S + S], xin[:, k * P:k * P + P], ident[:, :])
                    if j[0] == "stack":
                        w = j[1]
                        ended(pe, "proj", w, b)
                        for k in range(KB):
                            last = pe.transpose(ps[:, k * S:k * S + S], kq[:, k * P:k * P + P], ident[:, :])
                    if j[0] == "shift":
                        pe.wait_ge(nm_ready, 2 * (2 * j[1] + j[2]) + 2)
                        last = pe.transpose(ps[0:64, 0:S], nm[:, :, :, :].rearrange("p m s h -> p (m s h)").bitcast(F32),
                                            ident[:, :])
                    if j[0] == "norm_out":
                        _, b, c = j
                        pe.wait_ge(reg_ready, REG * b + (RC, REG)[c])
                        for r in range(*((0, RC), (RC, REG))[c]):
                            last = pe.transpose(ps[:, (r - RC * c) * P:(r - RC * c + 1) * P], reg[r][:, :], ident[:, :])
                    if j[0] == "oT":
                        pe.wait_ge(on_ready, 3 * (b + 1))
                        for k in range(KB):
                            last = pe.transpose(ps[:, k * S:k * S + S], on[:, k * P:k * P + P], ident[:, :])
                    if j[0] == "x2T":
                        pe.wait_ge(x2n_ready, b + 1)
                        for k in range(KB):
                            last = pe.transpose(ps[:, k * S:k * S + S], on[:, k * P:k * P + P], ident[:, :])
                    if j[0] == "out":
                        ended(pe, "oT", b)
                        pe.wait_ge(wo_low, 1)
                        last = product(ps, lambda p, i: (oTH, oTL)[p][:, i, :],
                                       lambda p, i: (WH, WL)[p][3][:, i, :], KB)
                    last.then_inc(job_ready, 1)
                e = g - LAG_B
                if 0 <= e < B * H:
                    b, h = divmod(e, H)
                    if h == 0:
                        pe.wait_ge(stack_in[KW][b % KST], 16 * (b // KST + 1))
                    if h % GH == 0:
                        pe.wait_ge(bd_built[QW], M * (e // GH + 1))
                    if h % HALF == 0:
                        ended(pe, "shift", b, h // HALF)
                        pe.wait_ge(dve_setup, 5)
                    since(pe, exp_ready, e - 1)
                    pe.matmul(PS[:, 2 + e % 2, :], Kst[b % KST][:, h, :],
                              Qbd[e // GH % 2][:, h % GH].rearrange("p m t -> p (m t)"), start=True, stop=False)
                    pe.matmul(PS[:, 2 + e % 2, :], sel[:, h % HALF, :],
                              nmbd[e // HALF % 2][:, :, :].rearrange("p m t -> p (m t)"),
                              start=False, stop=True).then_inc(b_ready, 1)
                v = g - LAG_V
                if 0 <= v < B * H:
                    b, h = divmod(v, H)
                    r, i = divmod(h, PER)
                    rg = REG * b + r
                    if h == 0:
                        ended(pe, "proj", VW, b)
                    if rg < 2 and i == 0:
                        ended(pe, *order[max(n for n in range(first_jobs) if BANK[n] == 4 + rg)])
                    if i == 0:
                        since(pe, reg_ready, rg - 1)
                    pe.wait_ge(exp_ready, v + 1)
                    for m in range(M):
                        last = pe.matmul(PS[32 * m:32 * m + 32, 4 + rg % 2, 0:S], Vpad[b % 2][:, h, m, :],
                                         PT[v % PTN][:, m, :], start=(i == 0), stop=(h == region_last(r)),
                                         tile_position=(0, 32 * m))
                    last.then_inc(v_ready, 1)

            def down(n):
                half, j = divmod(n, FB)
                mj = min(P, F - j * P)
                pe.wait_ge(hL_ready, n + 1)
                for t in range(4):
                    if j == 0 and half:
                        pe.wait_ge(y_added, t + 1)
                    for k, (a, c) in enumerate(((hH, dH), (hH, dL), (hL, dH))):
                        last = pe.matmul(PS[:, 4 + t, :], a[n % 2][0:mj, t * S:t * S + S], c[j][0:mj, :],
                                         start=(j == 0 and k == 0), stop=(j == FB - 1 and k == 2))
                    if j == FB - 1 or t == 3:
                        last.then_inc(y_ready, 1)

            pe.wait_ge(reg_ready, REG * B)
            ended(pe, *order[-2])
            ended(pe, *order[-1])
            for n in range(LEAD, 2 * FB):
                down(n - LEAD)
                for up in range(2):
                    gate_or_up(n, up)
            for n in range(2 * FB - LEAD, 2 * FB):
                down(n)


_OUTS = [((B, S, D), "float32")]


def kernel(**inputs):
    import numpy as _np
    import concourse.bacc as _bacc
    from concourse import mybir as _mybir
    from concourse.bass_utils import run_bass_kernel_spmd as _run

    a = {k: _np.asarray(v) for k, v in inputs.items()}
    rows = [h * M * DK + d * M + m
            for r in range(REG) for m in range(M) for h in range(PER * r, min(PER * r + PER, H)) for d in range(DK)]
    column = lambda v: v.reshape(KB, P).T
    laid = {
        "x": a["x"],
        "ctxT": a["ctx_4096"].transpose(0, 2, 1),
        "Wq": a["L0_xattn_Wq"], "Wk": a["L0_xattn_Wk"], "Wv": a["L0_xattn_Wv"],
        "WoT": a["L0_xattn_Wo"].T[rows],
        "bq": column(a["L0_xattn_bq"]), "bk": column(a["L0_xattn_bk"]), "bv": column(a["L0_xattn_bv"]),
        "bo": _np.broadcast_to(a["L0_xattn_bo"], (P, D)),
        "mix": _np.broadcast_to(a["L0_xattn_interference"][:, None], (H, DK, M, M)).reshape(H * DK * M, M),
        "amp": _np.broadcast_to(a["L0_xattn_amp"], (P, 1)),
        "WgT": a["L0_ffn_W_gate"].T, "WuT": a["L0_ffn_W_up"].T, "WdT": a["L0_ffn_W_down"].T,
    }
    nc = _bacc.Bacc("TRN2", target_bir_lowering=False, num_devices=1)
    arrays, args = {}, {}
    for name, v in laid.items():
        v = _np.ascontiguousarray(v)
        arrays[f"in_{name}_dram"] = v
        args[name] = nc.dram_tensor(f"in_{name}_dram", v.shape, _mybir.dt.from_np(v.dtype), kind="ExternalInput").ap()
    for i, (shape, dtype) in enumerate(_OUTS):
        args["out"] = nc.dram_tensor(f"out_{i}_dram", shape, _mybir.dt.from_np(_np.dtype(dtype)),
                                     kind="ExternalOutput").ap()
    build(nc, **args)
    r = _run(nc, [arrays], core_ids=[0])
    return r.results[0]["out_0_dram"]
```
